# Optimizing a Trainium2 kernel written in Bass

```python
import numpy as np
import jax
import jax.numpy as jnp

def _softmax(x, axis=-1):
    return jax.nn.softmax(x, axis=axis)
def _gelu(x):
    return jax.nn.gelu(x, approximate=True)
def _silu(x):
    return jax.nn.silu(x)
def _sigmoid(x):
    return jax.nn.sigmoid(x)
def _layernorm(x, axis=-1, eps=1e-5):
    m = jnp.mean(x, axis=axis, keepdims=True)
    v = jnp.var(x, axis=axis, keepdims=True)
    return (x - m) / jnp.sqrt(v + eps)
def _scatter_add(tgt, idx, src, axis=0):
    return tgt.at[idx].add(src)
def _segment_sum(src, seg, n):
    return jax.ops.segment_sum(src, seg, n)

kernel_name = 'mk_conv_seq_d1_conv_nhwc512_d904c1'

def setup_inputs(seed: int = 0):
    np.random.seed(seed)
    _w = jnp.asarray
    def _rec_inputs():
        import jax
        import jax.numpy as jnp
        _gk = jax.random.key(seed)
        x = 7.22e-05 + 1 * jax.random.normal(jax.random.fold_in(_gk, 1), (16, 32, 32, 512), jnp.float32)
        return x
    x = _rec_inputs()
    def _L0_conv_setup():
        import jax, jax.numpy as jnp
        import numpy as np
        N_HEADS = 8
        GROUPS = 32
        EPS = 1e-06

        def _group_norm(x, scale, bias):
            B, T, C = x.shape
            xg = x.reshape(B, T, GROUPS, C // GROUPS)
            mean = xg.mean(axis=(1, 3), keepdims=True)
            var = xg.var(axis=(1, 3), keepdims=True)
            xg = (xg - mean) * jax.lax.rsqrt(var + EPS)
            return xg.reshape(B, T, C) * scale + bias

        def _qkv_attention(qkv):
            bs, length, width = qkv.shape
            ch = width // (3 * N_HEADS)
            q, k, v = jnp.split(qkv, 3, axis=-1)
            scale = 1.0 / np.sqrt(np.sqrt(ch))
            q = (q * scale).reshape(bs * N_HEADS, length, ch)
            k = (k * scale).reshape(bs * N_HEADS, length, ch)
            v = v.reshape(bs * N_HEADS, length, ch)
            weight = jnp.einsum('btc,bsc->bts', q, k)
            weight = jax.nn.softmax(weight.astype(jnp.float32), axis=-1).astype(qkv.dtype)
            a = jnp.einsum('bts,bsc->btc', weight, v)
            return a.reshape(bs, length, -1)
        key = jax.random.key(seed)
        ks = jax.random.split(key, 4)
        B, H, W, C = (16, 32, 32, 512)
        x = jax.random.normal(ks[0], (B, H, W, C), dtype=jnp.float32)
        norm_scale = jnp.ones((C,), dtype=jnp.float32)
        norm_bias = jnp.zeros((C,), dtype=jnp.float32)
        qkv_w = jax.random.normal(ks[1], (C, 3 * C), dtype=jnp.float32) / np.sqrt(C)
        qkv_b = jax.random.normal(ks[2], (3 * C,), dtype=jnp.float32) * 0.02
        proj_w = jax.random.normal(ks[3], (C, C), dtype=jnp.float32) / np.sqrt(C)
        proj_b = jnp.zeros((C,), dtype=jnp.float32)
        return {'x': x, 'norm_scale': norm_scale, 'norm_bias': norm_bias, 'qkv_w': qkv_w, 'qkv_b': qkv_b, 'proj_w': proj_w, 'proj_b': proj_b}
    _L0_conv_all = _L0_conv_setup()
    _L0_conv_in = {k: v for k, v in _L0_conv_all.items() if k in ('norm_scale', 'norm_bias', 'qkv_w', 'qkv_b', 'proj_w', 'proj_b', )}
    del _L0_conv_all

    return {
        "x": x,
        "L0_conv_norm_scale": _L0_conv_in["norm_scale"],
        "L0_conv_norm_bias": _L0_conv_in["norm_bias"],
        "L0_conv_qkv_w": _L0_conv_in["qkv_w"],
        "L0_conv_qkv_b": _L0_conv_in["qkv_b"],
        "L0_conv_proj_w": _L0_conv_in["proj_w"],
        "L0_conv_proj_b": _L0_conv_in["proj_b"],
    }

def reference(x, L0_conv_norm_scale, L0_conv_norm_bias, L0_conv_qkv_w, L0_conv_qkv_b, L0_conv_proj_w, L0_conv_proj_b):
    import jax
    import jax.numpy as jnp
    def _L0_conv_ref(x, norm_scale, norm_bias, qkv_w, qkv_b, proj_w, proj_b):
        import jax, jax.numpy as jnp
        import numpy as np
        N_HEADS = 8
        GROUPS = 32
        EPS = 1e-06

        def _group_norm(x, scale, bias):
            B, T, C = x.shape
            xg = x.reshape(B, T, GROUPS, C // GROUPS)
            mean = xg.mean(axis=(1, 3), keepdims=True)
            var = xg.var(axis=(1, 3), keepdims=True)
            xg = (xg - mean) * jax.lax.rsqrt(var + EPS)
            return xg.reshape(B, T, C) * scale + bias

        def _qkv_attention(qkv):
            bs, length, width = qkv.shape
            ch = width // (3 * N_HEADS)
            q, k, v = jnp.split(qkv, 3, axis=-1)
            scale = 1.0 / np.sqrt(np.sqrt(ch))
            q = (q * scale).reshape(bs * N_HEADS, length, ch)
            k = (k * scale).reshape(bs * N_HEADS, length, ch)
            v = v.reshape(bs * N_HEADS, length, ch)
            weight = jnp.einsum('btc,bsc->bts', q, k)
            weight = jax.nn.softmax(weight.astype(jnp.float32), axis=-1).astype(qkv.dtype)
            a = jnp.einsum('bts,bsc->btc', weight, v)
            return a.reshape(bs, length, -1)
        b = x.shape[0]
        spatial = x.shape[1:-1]
        c = x.shape[-1]
        xf = x.reshape(b, -1, c)
        h = _group_norm(xf, norm_scale, norm_bias)
        qkv = h @ qkv_w + qkv_b
        h = _qkv_attention(qkv)
        h = h @ proj_w + proj_b
        return (xf + h).reshape(b, *spatial, c)

    def _gn(v, G=32, eps=1e-5):
        B_, H_, W_, C_ = v.shape
        g = v.reshape(B_, H_, W_, G, C_ // G)
        m = jnp.mean(g, axis=(1, 2, 4), keepdims=True)
        s = jnp.var(g, axis=(1, 2, 4), keepdims=True)
        return ((g - m) / jnp.sqrt(s + eps)).reshape(v.shape)

    def _ln_c(v, eps=1e-6):
        m = jnp.mean(v, axis=-1, keepdims=True)
        s = jnp.var(v, axis=-1, keepdims=True)
        return (v - m) / jnp.sqrt(s + eps)

    def _ln_t(v, eps=1e-5):
        m = jnp.mean(v, axis=-1, keepdims=True)
        s = jnp.var(v, axis=-1, keepdims=True)
        return (v - m) / jnp.sqrt(s + eps)

    def _to_tokens(v):
        B_, H_, W_, C_ = v.shape
        return v.reshape(B_, H_ * W_, C_)
    def _from_tokens(t, like):
        return t.reshape(like.shape)

    x = _L0_conv_ref(x, L0_conv_norm_scale, L0_conv_norm_bias, L0_conv_qkv_w, L0_conv_qkv_b, L0_conv_proj_w, L0_conv_proj_b)
    return x


_drawn_inputs = setup_inputs


def setup_inputs(seed=0):
    import zlib

    import numpy as np

    out = dict(_drawn_inputs(seed))
    spreads = {'L0_conv_norm_scale': (1.0, 0.6),
     'L0_conv_norm_bias': (0.0, 0.1),
     'L0_conv_proj_b': (0.0, 0.1)}
    factors = {'L0_conv_qkv_b': 8.0}
    for name, (base, spread) in spreads.items():
        noise = np.random.default_rng([zlib.crc32(name.encode()), seed]).standard_normal(out[name].shape)
        drawn = base * np.exp(spread * noise) if base else spread * noise
        out[name] = jnp.asarray(drawn.astype(out[name].dtype))
    for name, factor in factors.items():
        out[name] = (out[name] * factor).astype(out[name].dtype)
    return out
```

```python
from contextlib import ExitStack

import concourse.bass as bass
from concourse import mybir

F32 = mybir.dt.float32
F32R = mybir.dt.float32r
ALU = mybir.AluOpType
ACT = mybir.ActivationFunctionType
AX = mybir.AxisListType

P = 128
BATCHES, TOKENS, C = 16, 1024, 512
BLOCKS = TOKENS // P
CH = 64
CHUNKS = C // CH
NPOS = P * CHUNKS
KT = C // P
GROUP = C // 32
EPS = 1e-6
SPB = BLOCKS * CHUNKS
N_SLOTS = BATCHES * SPB
N_BLOCKS = BATCHES * BLOCKS
N_HALVES = 2 * N_BLOCKS
N_PAIRS = N_BLOCKS // 2
PPB = BLOCKS // 2
XRING = 4

STAT_SLOTS = [2, 4, 6, 9, 17, 20, 22, 25]
AGGREGATE_SLOT = 29
GROUP_MEAN_SLOT = 33
GROUP_VAR_SLOT = 36


def within(n, count):
    return not isinstance(n, int) or 0 <= n < count


def at_least(engine, sem, count):
    if not isinstance(count, int) or count > 0:
        engine.wait_ge(sem, count)


def large_unit(k):
    m = k % 16
    if m % 8 < 2:
        return "proj", 0, m % 8
    if m < 8:
        return "qk", m - 2, 0
    if m < 12:
        return "qk", m - 4, 0
    return "v", (m - 12) // 2, m % 2


def small_unit(k):
    m = k % 16
    if m % 4 == 3:
        return "spread", 0
    if m in (10, 13):
        return "xt", (m - 10) // 3
    if k in STAT_SLOTS:
        return "stats", STAT_SLOTS.index(k)
    if k == GROUP_MEAN_SLOT:
        return "group", 0
    if k == GROUP_VAR_SLOT:
        return "group", 1
    return None, 0


def attention_block(nc, x, norm_scale, norm_bias, qkv_w, qkv_b, proj_w, proj_b, out):
    x_t = x.rearrange("b h w c -> b (h w) c").rearrange("b (n t) c -> b n t c", t=P)
    out_t = out.rearrange("b h w c -> b (h w) c").rearrange("b (n t) c -> b n t c", t=P)

    with ExitStack() as ctx:
        def sb(name, shape, dt=F32):
            return ctx.enter_context(nc.sbuf_tensor(name, shape, dt))

        def ps(name, shape):
            return ctx.enter_context(nc.psum_tensor(name, shape, F32))

        def sem(name):
            return ctx.enter_context(nc.semaphore(name))

        w_hi = sb("w_hi", [P, KT, 3 * C], F32R)
        w_lo = sb("w_lo", [P, KT, 3 * C], F32R)
        pw_hi = sb("pw_hi", [P, KT, C], F32R)
        pw_lo = sb("pw_lo", [P, KT, C], F32R)
        h_norm = sb("h_norm", [P, KT, 2 * P])
        h_hi = sb("h_hi", [P, KT, 2 * P], F32R)
        h_lo = sb("h_lo", [P, KT, 2 * P], F32R)
        x_pair = sb("x_pair", [P, XRING, 2, C])
        x_stat = sb("x_stat", [P, C])
        q_st = [[sb(f"q_{n}{g}", [P, 2, CHUNKS // 2, P], F32R) for n in "eo"] for g in range(2)]
        k_hi = [[sb(f"kh_{n}{g}", [P, 2, CHUNKS // 2, P], F32R) for n in "eo"] for g in range(2)]
        k_lo = [[sb(f"kl_{n}{g}", [P, 2, CHUNKS // 2, P], F32R) for n in "eo"] for g in range(2)]
        v_sb = [sb(f"v{g}", [P, 2, C]) for g in range(2)]
        probs = [sb(f"probs{i}", [P, NPOS]) for i in range(2)]
        probs_t = [sb(f"probs_t{i}", [P, CHUNKS, 4, P]) for i in range(2)]
        attn = sb("attn", [P, 2, 2 * P])
        attn_hi = sb("attn_hi", [P, 2, 2 * P], F32R)
        attn_lo = sb("attn_lo", [P, 2, 2 * P], F32R)
        inv_spread = sb("inv_spread", [P, 2 * P])
        v_bias = sb("v_bias", [P, C])
        p_bias = sb("p_bias", [P, C])
        ident = sb("ident", [P, P])
        group_avg = sb("group_avg", [P, P])
        qk_bias = sb("qk_bias", [P, 2 * KT])
        n_scale = sb("n_scale", [P, KT])
        n_bias = sb("n_bias", [P, KT])
        bn = sb("bn", [P, KT, BLOCKS, 6])
        mv = sb("mv", [P, KT, 2])
        gmv = sb("gmv", [P, KT, 2])
        dmean = sb("dmean", [P, KT])
        dsq = sb("dsq", [P, KT])
        gvar = sb("gvar", [P, KT])
        rstd = sb("rstd", [P, KT])
        mean_a = sb("mean_a", [P, KT])
        half_neg = sb("half_neg", [P, KT])
        x_mul = sb("x_mul", [P, KT])
        x_add = sb("x_add", [P, KT])
        neg_max = sb("neg_max", [P, 4])
        row_sum = [sb(f"row_sum{i}", [P, 4]) for i in range(2)]
        inv_sum = sb("inv_sum", [P, 4])
        inv_wide = sb("inv_wide", [P, 4, CH])

        s_ps = [ps(f"s_ps{i}", [P, NPOS]) for i in range(2)]
        t_ps = [ps(f"t_ps{i}", [P, 4, P]) for i in range(2)]
        pv_ps = ps("pv_ps", [P, 2, 2 * P])
        c_ps = ps("c_ps", [P, C])

        w_loaded = [sem(f"w_loaded{i}") for i in range(KT)]
        pw_loaded = sem("pw_loaded")
        const_loaded = sem("const_loaded")
        const_made = sem("const_made")
        w_ready = sem("w_ready")
        dve_chain = sem("dve_chain")
        pool_chain = sem("pool_chain")
        x_loaded = [sem(f"x_loaded{i}") for i in range(XRING)]
        stored = [sem(f"stored{i}") for i in range(XRING)]
        xs_loaded = sem("xs_loaded")
        stats_full = sem("stats_full")
        stats_taken = sem("stats_taken")
        aggregated = sem("aggregated")
        mean_off = sem("mean_off")
        group_full = sem("group_full")
        group_taken = sem("group_taken")
        affine_ready = sem("affine_ready")
        xt_full = sem("xt_full")
        xt_normed = sem("xt_normed")
        h_rounded = sem("h_rounded")
        h_split = sem("h_split")
        affine_step = sem("affine_step")
        residual_ready = sem("residual_ready")
        qk_full = sem("qk_full")
        qk_hi_done = sem("qk_hi_done")
        qk_ready = sem("qk_ready")
        v_full = sem("v_full")
        v_ready = sem("v_ready")
        scores_full = sem("scores_full")
        max_ready = sem("max_ready")
        probs_ready = sem("probs_ready")
        t_full = [sem(f"t_full{i}") for i in range(2)]
        t_taken = [sem(f"t_taken{i}") for i in range(2)]
        pv_done = sem("pv_done")
        inv_ready = sem("inv_ready")
        inv_widened = sem("inv_widened")
        spread_full = sem("spread_full")
        spread_taken = sem("spread_taken")
        attn_ready = sem("attn_ready")
        attn_hi_done = sem("attn_hi_done")
        attn_lo_done = sem("attn_lo_done")
        proj_full = sem("proj_full")
        out_ready = sem("out_ready")

        def proj_block(b, k):
            return BLOCKS * b + k // 8 - 2

        def spread_half(b, k):
            return 2 * BLOCKS * b + k // 4 - 1

        def made_pair(b, k):
            return PPB * b + k // 16 + 1

        def xt_pair(b, k):
            return PPB * b + k // 16 + 2

        tenants = []
        for k in range(SPB):
            if large_unit(k)[2] == 0:
                tenants.append((k, 0))
            if small_unit(k)[0]:
                tenants.append((k, 1))

        def emptied(b, k, small):
            kind, n = small_unit(k) if small else large_unit(k)[:2]
            if kind == "proj":
                h = proj_block(b, k)
                return within(h, N_BLOCKS), out_ready, h + 1
            if kind == "spread":
                half = spread_half(b, k)
                return within(half, N_HALVES), spread_taken, half + 1
            if kind == "qk":
                g = made_pair(b, k)
                return within(g, N_PAIRS), qk_ready, 2 * KT * g + n + 1
            if kind == "v":
                g = made_pair(b, k)
                return within(g, N_PAIRS), v_ready, 2 * g + n + 1
            if kind == "xt":
                g = xt_pair(b, k)
                return within(g, N_PAIRS), xt_normed, 2 * g + n + 1
            if kind == "stats":
                return within(b + 1, BATCHES), stats_taken, BLOCKS * (b + 1) + n + 1
            return within(b + 1, BATCHES), group_taken, 2 * (b + 1) + n + 1

        def await_shared_bank(pe, b, k, small):
            i = tenants.index((k, small))
            for back in range(1, len(tenants) + 1):
                bb = b if i - back >= 0 else b - 1
                if isinstance(bb, int) and bb < -1:
                    return
                exists, taken, count = emptied(bb, *tenants[i - back])
                if exists:
                    pe.wait_ge(taken, count)
                    return

        def batches(engine, slot):
            for b in (-1, 0):
                for k in range(SPB):
                    slot(b, k)
            with engine.Fori(1, BATCHES - 1) as b:
                for k in range(SPB):
                    slot(b, k)
            for k in range(SPB):
                slot(BATCHES - 1, k)
            for k in range(18):
                slot(BATCHES, k)

        def copy_transposed(engine, copy, b, k, grp):
            n = (k - 1) // 4
            t = SPB * b + k - 1
            engine.wait_ge(t_full[grp], t + 1)
            if (k - 1) % 4 == 0:
                at_least(engine, pv_done, 2 * BLOCKS * b + n - 1)
            copy(probs_t[n % 2][:, 4 * grp:4 * grp + 4, (k - 1) % 4, :], t_ps[grp][:, :, :]).then_inc(t_taken[grp], 1)

        def at_least_aside(engine, sem, count):
            if isinstance(count, int):
                return at_least(engine, sem, count)
            engine.compute_val(count)
            engine.wait_ge(const_made, 2)
            engine.wait_ge(sem, count)

        block = ctx.enter_context(nc.Block())

        @block.sync
        def _(sp):
            for t in range(KT):
                stage = probs_t[t // 2][:, 3 * (t % 2):3 * (t % 2) + 3, :, :].rearrange("p a b c -> p (a b c)")
                sp.dma_start(stage, qkv_w[t * P:(t + 1) * P, :]).then_inc(w_loaded[t], 16)
            for t in range(KT):
                sp.dma_start(probs[t // 2][:, (t % 2) * C:(t % 2 + 1) * C],
                             proj_w[t * P:(t + 1) * P, :]).then_inc(pw_loaded, 16)

            def load_stat_tile(b, u):
                if within(b + 1, BATCHES):
                    at_least_aside(sp, stats_full, BLOCKS * (b + 1) + u)
                    sp.dma_start(x_stat[:, :], x_t[b + 1, u]).then_inc(xs_loaded, 16)

            def slot(b, k):
                if k % 8 == 1:
                    h = proj_block(b, k)
                    n = (k - 1) // 8 - 2
                    if within(h, N_BLOCKS):
                        at_least_aside(sp, out_ready, h + 1)
                        ring = (n // 2) % XRING
                        sp.dma_start(out_t[b + n // BLOCKS, n % BLOCKS],
                                     x_pair[:, ring, n % 2, :]).then_inc(stored[ring], 16)
                if k % 16 == 2:
                    g = xt_pair(b, k)
                    n = k // 16 + 2
                    if within(g, N_PAIRS):
                        at_least_aside(sp, stored[n % XRING], 32 * (b + n // PPB))
                        first = 2 * (n % PPB)
                        sp.dma_start(x_pair[:, n % XRING, :, :],
                                     x_t[b + n // PPB, first:first + 2].rearrange("n t c -> t n c")
                                     ).then_inc(x_loaded[n % XRING], 16)
                if k == 0:
                    load_stat_tile(b, 0)
                if k in STAT_SLOTS[:-1]:
                    load_stat_tile(b, STAT_SLOTS.index(k) + 1)

            batches(sp, slot)
            for ring in range(XRING):
                sp.wait_ge(stored[ring], 16 * N_BLOCKS // XRING)

        @block.tensor
        def _(pe):
            def scores(b, k):
                s = SPB * b + k
                g, i, c, buf = PPB * b + k // 16, (k // 8) % 2, k % 8, (k // 16) % 2
                if k % 16 == 0:
                    pe.wait_ge(qk_ready, 2 * KT * (g + 1))
                if within(s - 2, N_SLOTS):
                    pe.wait_ge(probs_ready, s - 1)
                q = q_st[buf][c % 2][:, i, c // 2, :]
                for par in range(2):
                    dst = s_ps[k % 2][:, par * C:(par + 1) * C]
                    nc.tensor.matmul(dst, q, k_hi[buf][par][:, i, :, :].rearrange("p j t -> p (j t)"),
                                     start=True, stop=False)
                    last = nc.tensor.matmul(dst, q, k_lo[buf][par][:, i, :, :].rearrange("p j t -> p (j t)"),
                                            start=False, stop=True)
                last.then_inc(scores_full, 1)

            def transposes(b, k):
                t = SPB * b + k - 1
                pe.wait_ge(probs_ready, t + 1)
                for grp in range(2):
                    at_least(pe, t_taken[grp], t)
                    for n in range(4):
                        kt = 4 * grp + n
                        last = nc.tensor.transpose(t_ps[grp][:, n, :], probs[(k - 1) % 2][:, kt * P:(kt + 1) * P],
                                                   ident[:, :])
                    last.then_inc(t_full[grp], 1)

            def attend(b, k):
                n, part = (k - 5) // 4, (k - 5) % 4
                half = 2 * BLOCKS * b + n
                i, buf, side = (n // 2) % 2, (n // 4) % 2, n % 2
                if part == 0:
                    for grp in range(2):
                        pe.wait_ge(t_taken[grp], 4 * half + 4)
                    if n % 4 == 0:
                        pe.wait_ge(v_ready, 2 * (PPB * b + n // 4) + 2)
                    at_least(pe, attn_ready, half)
                for kt in (2 * part, 2 * part + 1):
                    chunk = 2 * (kt % 4) + kt // 4
                    for par in range(2):
                        last = nc.tensor.matmul(
                            pv_ps[CH * par:CH * (par + 1), side, :],
                            v_sb[buf][:, i, CH * chunk:CH * (chunk + 1)],
                            probs_t[side][:, kt, :, :].rearrange("p (a r) t -> p r a t", r=2)[:, par, :, :],
                            start=(kt == 0), stop=(kt == 7))
                if part == 3:
                    last.then_inc(pv_done, 1)

            def large(b, k):
                kind, n, part = large_unit(k)
                if kind == "proj":
                    h = proj_block(b, k)
                    if not within(h, N_BLOCKS):
                        return
                    if part == 0:
                        pe.wait_ge(attn_hi_done, 2 * h + 2)
                        pe.wait_ge(attn_lo_done, 2 * h + 2)
                        await_shared_bank(pe, b, k, 0)
                    for j in (2 * part, 2 * part + 1):
                        a_hi = attn_hi[:, j // 2, (j % 2) * P:(j % 2 + 1) * P]
                        a_lo = attn_lo[:, j // 2, (j % 2) * P:(j % 2 + 1) * P]
                        nc.tensor.matmul(c_ps[:, :], a_hi, pw_hi[:, j, :], start=(j == 0), stop=False)
                        nc.tensor.matmul(c_ps[:, :], a_hi, pw_lo[:, j, :], start=False, stop=False)
                        last = nc.tensor.matmul(c_ps[:, :], a_lo, pw_hi[:, j, :], start=False, stop=(j == 3))
                    if part == 1:
                        last.then_inc(proj_full, 1)
                    return
                g = made_pair(b, k)
                if not within(g, N_PAIRS):
                    return
                if kind == "qk":
                    if n == 0:
                        pe.wait_ge(h_split, 2 * g + 2)
                    await_shared_bank(pe, b, k, 0)
                    for t in range(KT):
                        wh, wl = (w[:, t, n * P:(n + 1) * P] for w in (w_hi, w_lo))
                        nc.tensor.matmul(c_ps[:, 0:2 * P], wh, h_hi[:, t, :], start=(t == 0), stop=False)
                        nc.tensor.matmul(c_ps[:, 0:2 * P], wh, h_lo[:, t, :], start=False, stop=False)
                        last = nc.tensor.matmul(c_ps[:, 0:2 * P], wl, h_hi[:, t, :], start=False, stop=(t == KT - 1))
                    last.then_inc(qk_full, 1)
                else:
                    if part == 0:
                        await_shared_bank(pe, b, k, 0)
                    for t in (2 * part, 2 * part + 1):
                        hh, hl = (h[:, t, n * P:(n + 1) * P] for h in (h_hi, h_lo))
                        nc.tensor.matmul(c_ps[:, :], hh, w_hi[:, t, 2 * C:3 * C], start=(t == 0), stop=False)
                        nc.tensor.matmul(c_ps[:, :], hh, w_lo[:, t, 2 * C:3 * C], start=False, stop=False)
                        last = nc.tensor.matmul(c_ps[:, :], hl, w_hi[:, t, 2 * C:3 * C], start=False, stop=(t == KT - 1))
                    if part == 1:
                        last.then_inc(v_full, 1)

            def small(b, k):
                kind, n = small_unit(k)
                if kind is None or not emptied(b, k, 1)[0]:
                    return
                if kind == "stats":
                    pe.wait_ge(xs_loaded, 16 * (BLOCKS * (b + 1) + n + 1))
                    await_shared_bank(pe, b, k, 1)
                    for t in range(KT):
                        last = nc.tensor.transpose(c_ps[:, t * P:(t + 1) * P], x_stat[:, t * P:(t + 1) * P], ident[:, :])
                    last.then_inc(stats_full, 1)
                elif kind == "group":
                    pe.wait_ge(aggregated, 2 * (b + 1) + n + 1)
                    await_shared_bank(pe, b, k, 1)
                    src = mv[:, :, :].rearrange("p t s -> p (t s)") if n == 0 else dsq[:, :]
                    nc.tensor.matmul(c_ps[:, 0:(2 - n) * KT], group_avg[:, :], src,
                                     start=True, stop=True).then_inc(group_full, 1)
                elif kind == "xt":
                    ring = (k // 16 + 2) % XRING
                    if n == 0:
                        pe.wait_ge(x_loaded[ring], 16 * (b + (k // 16 + 2) // PPB + 1))
                    await_shared_bank(pe, b, k, 1)
                    for t in range(2):
                        for i in range(2):
                            last = nc.tensor.transpose(c_ps[:, (2 * t + i) * P:(2 * t + i + 1) * P],
                                                       x_pair[:, ring, i, (2 * n + t) * P:(2 * n + t + 1) * P],
                                                       ident[:, :])
                    last.then_inc(xt_full, 1)
                else:
                    pe.wait_ge(inv_widened, spread_half(b, k) + 1)
                    await_shared_bank(pe, b, k, 1)
                    for j in range(2):
                        inv = inv_wide[:, 2 * j:2 * j + 2, :].rearrange("p c n -> p (c n)")
                        last = nc.tensor.transpose(c_ps[:, j * P:(j + 1) * P], inv, ident[:, :])
                    last.then_inc(spread_full, 1)

            def slot(b, k):
                s = SPB * b + k
                if within(s, N_SLOTS):
                    scores(b, k)
                large(b, k)
                if within(s - 5, N_SLOTS):
                    attend(b, k)
                small(b, k)
                if within(s - 1, N_SLOTS):
                    transposes(b, k)

            pe.wait_ge(const_made, 2)
            pe.wait_ge(w_ready, 2 * KT)
            batches(pe, slot)

        @block.scalar
        def _(act):
            def softmax_exp(b, k):
                s = SPB * b + k
                half, c = 2 * BLOCKS * b + k // 4, k % 4
                act.wait_ge(max_ready, s + 1)
                if within(s - 2, N_SLOTS):
                    act.wait_ge(t_full[1], s - 1)
                if c == 0 and within(half - 2, N_HALVES):
                    act.wait_ge(inv_ready, half - 1)
                nc.scalar.activation(probs[k % 2][:, :], s_ps[k % 2][:, :], ACT.Exp,
                                     bias=neg_max[:, k % 4:k % 4 + 1],
                                     accum_out=row_sum[(k // 4) % 2][:, c:c + 1]).then_inc(probs_ready, 1)

            def qk_hi(b, k, n):
                g, buf, j = made_pair(b, k), (k // 16 + 1) % 2, n % KT
                act.wait_ge(qk_full, 2 * KT * g + n + 1)
                if n == 0 and within(g - 2, N_PAIRS):
                    act.wait_ge(scores_full, 16 * (g - 1))
                low, high = slice(0, CH), slice(CH, P)
                if n < KT:
                    places = ((q_st[buf][0], low, low), (q_st[buf][1], high, high))
                else:
                    places = ((k_hi[buf][0], low, low), (k_hi[buf][0], high, low),
                              (k_hi[buf][1], high, high), (k_hi[buf][1], low, high))
                for dst, to, of in places:
                    last = nc.scalar.activation(dst[to, :, j, :], c_ps[of, 0:2 * P].rearrange("p (i t) -> p i t", i=2),
                                                ACT.Identity, bias=qk_bias[of, n:n + 1])
                last.then_inc(qk_hi_done, 1)

            def norm_x(b, k, n):
                g = xt_pair(b, k)
                act.wait_ge(xt_full, 2 * g + n + 1)
                if k == 2 * 16 + 10:
                    act.wait_ge(affine_ready, b + 2)
                if within(g - 1, N_PAIRS):
                    act.wait_ge(h_split, 2 * g)
                for t in range(2):
                    ct = 2 * n + t
                    last = nc.scalar.activation(h_norm[:, ct, :], c_ps[:, 2 * t * P:2 * (t + 1) * P], ACT.Identity,
                                                bias=x_add[:, ct:ct + 1], scale=x_mul[:, ct:ct + 1])
                last.then_inc(xt_normed, 1)

            def slot(b, k):
                s = SPB * b + k
                if within(s, N_SLOTS):
                    softmax_exp(b, k)
                kind, n, _ = large_unit(k)
                if kind == "qk" and within(made_pair(b, k), N_PAIRS):
                    qk_hi(b, k, n)
                kind, n = small_unit(k)
                if kind == "xt" and within(xt_pair(b, k), N_PAIRS):
                    norm_x(b, k, n)
                if kind == "spread" and within(spread_half(b, k), N_HALVES):
                    half = spread_half(b, k)
                    act.wait_ge(spread_full, half + 1)
                    at_least(act, attn_ready, half)
                    nc.scalar.copy(inv_spread[:, :], c_ps[:, 0:2 * P]).then_inc(spread_taken, 1)
                if k % 4 == 1:
                    half, side = 2 * BLOCKS * b + k // 4 - 2, (k // 4) % 2
                    if within(half, N_HALVES):
                        act.wait_ge(attn_ready, half + 1)
                        at_least(act, proj_full, BLOCKS * b + k // 8 - 1)
                        nc.scalar.copy(attn_hi[:, side, :], attn[:, side, :]).then_inc(attn_hi_done, 1)
                if within(s - 1, N_SLOTS):
                    copy_transposed(act, nc.scalar.copy, b, k, 0)

            act.wait_ge(const_loaded, 16 * 5)
            act.wait_ge(dve_chain, 1)
            batches(act, slot)

        @block.vector
        def _(dve):
            dve.wait_ge(const_loaded, 16 * 5)
            nc.vector.tensor_scalar(qk_bias[:, KT:2 * KT], qk_bias[:, KT:2 * KT], CH ** -0.5, None,
                                    ALU.mult).then_inc(dve_chain, 1)
            chain = 1
            for t in range(KT):
                w = probs_t[t // 2][:, 3 * (t % 2):3 * (t % 2) + 3, :, :].rearrange("p a b c -> p (a b c)")
                dve.wait_ge(w_loaded[t], 16)
                nc.vector.tensor_scalar(w[:, C:2 * C], w[:, C:2 * C], CH ** -0.5, None, ALU.mult).then_inc(dve_chain, 1)
                chain += 1
                dve.wait_ge(dve_chain, chain)
                nc.vector.tensor_copy(w_hi[:, t, :], w).then_inc(dve_chain, 1)
                chain += 1
                dve.wait_ge(dve_chain, chain)
                nc.vector.tensor_tensor(w_lo[:, t, :], w, w_hi[:, t, :].bitcast(F32), ALU.subtract).then_inc(w_ready, 1)
            dve.wait_ge(pw_loaded, 16 * KT)
            for t in range(KT):
                w = probs[t // 2][:, (t % 2) * C:(t % 2 + 1) * C]
                nc.vector.tensor_copy(pw_hi[:, t, :], w).then_inc(dve_chain, 1)
                chain += 1
                dve.wait_ge(dve_chain, chain)
                nc.vector.tensor_tensor(pw_lo[:, t, :], w, pw_hi[:, t, :].bitcast(F32), ALU.subtract).then_inc(w_ready, 1)

            def qk_split(b, k, n):
                g, buf, j = made_pair(b, k), (k // 16 + 1) % 2, n % KT
                dve.wait_ge(qk_hi_done, 2 * KT * g + n + 1)
                low, high = slice(0, CH), slice(CH, P)
                if n < KT:
                    places = ((q_st[buf][0], high, low, q_st[buf][0]), (q_st[buf][1], low, high, q_st[buf][1]))
                else:
                    places = ((k_lo[buf][0], low, low, k_hi[buf][0]), (k_lo[buf][0], high, low, k_hi[buf][0]),
                              (k_lo[buf][1], high, high, k_hi[buf][1]), (k_lo[buf][1], low, high, k_hi[buf][1]))
                for dst, to, of, hi in places:
                    last = nc.vector.scalar_tensor_tensor(
                        dst[to, :, j, :], c_ps[of, 0:2 * P].rearrange("p (i t) -> p i t", i=2), qk_bias[of, n:n + 1],
                        hi[of, :, j, :].bitcast(F32), ALU.add, ALU.subtract)
                last.then_inc(qk_ready, 1)

            def slot(b, k):
                s = SPB * b + k
                if within(s, N_SLOTS):
                    dve.wait_ge(scores_full, s + 1)
                    nc.vector.tensor_reduce(neg_max[:, k % 4:k % 4 + 1], s_ps[k % 2][:, :], AX.X, ALU.max,
                                            negate=True).then_inc(max_ready, 1)
                if k % 4 == 0:
                    half = 2 * BLOCKS * b + k // 4 - 1
                    if within(half, N_HALVES):
                        dve.wait_ge(probs_ready, 4 * half + 4)
                        at_least(dve, inv_widened, half)
                        nc.vector.reciprocal(inv_sum[:, :], row_sum[(k // 4 - 1) % 2][:, :]).then_inc(inv_ready, 1)
                kind, n, part = large_unit(k)
                if kind == "qk" and within(made_pair(b, k), N_PAIRS):
                    qk_split(b, k, n)
                if kind == "v" and part == 1 and within(made_pair(b, k), N_PAIRS):
                    g = made_pair(b, k)
                    dve.wait_ge(v_full, 2 * g + n + 1)
                    if n == 0 and within(g - 2, N_PAIRS):
                        dve.wait_ge(pv_done, 4 * (g - 1))
                    nc.vector.tensor_tensor(v_sb[(k // 16 + 1) % 2][:, n, :], c_ps[:, :], v_bias[:, :],
                                            ALU.add).then_inc(v_ready, 1)
                if kind == "proj" and part == 1:
                    h, n = proj_block(b, k), k // 8 - 2
                    if within(h, N_BLOCKS):
                        dve.wait_ge(proj_full, h + 1)
                        if n % 2 == 0:
                            dve.wait_ge(residual_ready, PPB * b + n // 2 + 1)
                        r = x_pair[:, (n // 2) % XRING, n % 2, :]
                        nc.vector.tensor_tensor(r, c_ps[:, :], r, ALU.add).then_inc(out_ready, 1)
                statistics(b, k)
                if k % 4 == 0:
                    half, side = 2 * BLOCKS * b + k // 4 - 2, (k // 4) % 2
                    if within(half, N_HALVES):
                        dve.wait_ge(pv_done, half + 1)
                        dve.wait_ge(spread_taken, half + 1)
                        at_least(dve, attn_lo_done, half - 1)
                        nc.vector.tensor_tensor(attn[:, side, :], pv_ps[:, side, :], inv_spread[:, :],
                                                ALU.mult).then_inc(attn_ready, 1)
                if within(s - 1, N_SLOTS):
                    copy_transposed(dve, nc.vector.tensor_copy, b, k, 1)

            def statistics(b, k):
                if not within(b + 1, BATCHES):
                    return
                nb = b + 1
                if k in STAT_SLOTS:
                    u = STAT_SLOTS.index(k)
                    dve.wait_ge(stats_full, BLOCKS * nb + u + 1)
                    if u == 0:
                        at_least(dve, aggregated, 2 * nb)
                    for t in range(KT):
                        last = nc.vector.bn_stats(bn[:, t, u, :], c_ps[:, t * P:(t + 1) * P])
                    last.then_inc(stats_taken, 1)
                if k == AGGREGATE_SLOT:
                    at_least_aside(dve, stats_taken, BLOCKS * (nb + 1))
                    for t in range(KT):
                        last = nc.vector.bn_aggr(mv[:, t, :], bn[:, t, :, :].rearrange("p u s -> p (u s)"))
                    last.then_inc(aggregated, 1)
                if k == GROUP_MEAN_SLOT:
                    dve.wait_ge(group_full, 2 * nb + 1)
                    at_least(dve, affine_ready, nb)
                    nc.vector.tensor_copy(gmv[:, :, :].rearrange("p t s -> p (t s)"), c_ps[:, 0:2 * KT]).then_inc(group_taken, 1)
                    dve.wait_ge(group_taken, 2 * nb + 1)
                    nc.vector.tensor_tensor(dmean[:, :], mv[:, :, 0], gmv[:, :, 0], ALU.subtract).then_inc(mean_off, 1)
                    dve.wait_ge(mean_off, nb + 1)
                    nc.vector.tensor_tensor(dsq[:, :], dmean[:, :], dmean[:, :], ALU.mult).then_inc(aggregated, 1)
                if k == GROUP_VAR_SLOT:
                    dve.wait_ge(group_full, 2 * nb + 2)
                    nc.vector.scalar_tensor_tensor(gvar[:, :], c_ps[:, 0:KT], EPS, gmv[:, :, 1],
                                                   ALU.add, ALU.add).then_inc(group_taken, 1)

            batches(dve, slot)

        @block.gpsimd
        def _(pool):
            def broadcast_row(row):
                return row.rearrange("(a n) -> a n", a=1).broadcast_to([P, C])

            pool.dma_start(v_bias[:, :], broadcast_row(qkv_b[2 * C:3 * C])).then_inc(const_loaded, 16)
            pool.dma_start(p_bias[:, :], broadcast_row(proj_b)).then_inc(const_loaded, 16)
            with nc.allow_non_contiguous_dma("vectors to the partitions, once"):
                pool.dma_start(qk_bias[:, :], qkv_b[0:2 * C].rearrange("(j p) -> p j", p=P)).then_inc(const_loaded, 16)
                pool.dma_start(n_scale[:, :], norm_scale.rearrange("(j p) -> p j", p=P)).then_inc(const_loaded, 16)
                pool.dma_start(n_bias[:, :], norm_bias.rearrange("(j p) -> p j", p=P)).then_inc(const_loaded, 16)
            nc.gpsimd.memset(ident[:, :], 0.0).then_inc(pool_chain, 1)
            nc.gpsimd.memset(group_avg[:, :], 1.0 / GROUP).then_inc(pool_chain, 1)
            nc.gpsimd.memset(half_neg[:, :], -0.5).then_inc(pool_chain, 1)
            pool.wait_ge(pool_chain, 3)
            nc.gpsimd.affine_select(out=ident[:, :], in_=ident[:, :], compare_op=ALU.not_equal, fill=1.0, base=0,
                                    pattern=[[-1, P]], channel_multiplier=1).then_inc(const_made, 1)
            groups = group_avg[:, :].rearrange("p (g c) -> p g c", c=GROUP)
            nc.gpsimd.affine_select(out=groups, in_=groups, compare_op=ALU.is_ge, fill=0.0, base=0,
                                    pattern=[[-GROUP, P // GROUP], [0, GROUP]], channel_multiplier=1).then_inc(pool_chain, 1)
            pool.wait_ge(pool_chain, 4)
            nc.gpsimd.affine_select(out=groups, in_=groups, compare_op=ALU.is_ge, fill=0.0, base=GROUP - 1,
                                    pattern=[[GROUP, P // GROUP], [0, GROUP]], channel_multiplier=-1).then_inc(const_made, 1)
            pool.wait_ge(const_loaded, 16 * 5)

            def split_h(b, k):
                g = xt_pair(b, k)
                at_least_aside(pool, v_full, 2 * g)
                for n in range(2):
                    part = slice(2 * n, 2 * n + 2)
                    at_least_aside(pool, xt_normed, 2 * g + n + 1)
                    nc.gpsimd.tensor_copy(h_hi[:, part, :], h_norm[:, part, :]).then_inc(h_rounded, 1)
                    pool.wait_ge(h_rounded, 2 * g + n + 1)
                    nc.gpsimd.tensor_tensor(h_lo[:, part, :], h_norm[:, part, :], h_hi[:, part, :].bitcast(F32),
                                            ALU.subtract).then_inc(h_split, 1)

            def affine(b):
                nb = b + 1
                pool.wait_ge(group_taken, 2 * nb + 2)
                nc.gpsimd.tensor_tensor(rstd[:, :], gvar[:, :], half_neg[:, :], ALU.pow).then_inc(affine_step, 1)
                at_least(pool, xt_normed, 2 * PPB * nb)
                pool.wait_ge(affine_step, 3 * nb + 1)
                nc.gpsimd.tensor_tensor(x_mul[:, :], rstd[:, :], n_scale[:, :], ALU.mult).then_inc(affine_step, 1)
                pool.wait_ge(affine_step, 3 * nb + 2)
                nc.gpsimd.tensor_tensor(mean_a[:, :], gmv[:, :, 0], x_mul[:, :], ALU.mult).then_inc(affine_step, 1)
                pool.wait_ge(affine_step, 3 * nb + 3)
                nc.gpsimd.tensor_tensor(x_add[:, :], n_bias[:, :], mean_a[:, :], ALU.subtract).then_inc(affine_ready, 1)

            def slot(b, k):
                if k % 16 == 15 and within(xt_pair(b, k), N_PAIRS):
                    split_h(b, k)
                if k % 16 == 1:
                    g, n = made_pair(b, k), k // 16 + 1
                    if within(g, N_PAIRS):
                        pool.wait_ge(xt_full, 2 * g + 2)
                        for i in range(2):
                            r = x_pair[:, n % XRING, i, :]
                            last = nc.gpsimd.tensor_tensor(r, r, p_bias[:, :], ALU.add)
                        last.then_inc(residual_ready, 1)
                if k % 4 == 0:
                    half = 2 * BLOCKS * b + k // 4 - 1
                    if within(half, N_HALVES):
                        at_least_aside(pool, spread_full, half)
                        at_least_aside(pool, inv_ready, half + 1)
                        nc.gpsimd.tensor_copy(inv_wide[:, :, :], inv_sum[:, :].unsqueeze(2).broadcast_to([P, 4, CH])
                                              ).then_inc(inv_widened, 1)
                if k % 4 == 1:
                    half, side = 2 * BLOCKS * b + k // 4 - 2, (k // 4) % 2
                    if within(half, N_HALVES):
                        pool.wait_ge(attn_hi_done, half + 1)
                        at_least(pool, proj_full, BLOCKS * b + k // 8 - 1)
                        nc.gpsimd.tensor_tensor(attn_lo[:, side, :], attn[:, side, :], attn_hi[:, side, :].bitcast(F32),
                                                ALU.subtract).then_inc(attn_lo_done, 1)
                if k == GROUP_VAR_SLOT and within(b + 1, BATCHES):
                    affine(b)

            batches(pool, slot)


_INS = ["x", "L0_conv_norm_scale", "L0_conv_norm_bias", "L0_conv_qkv_w", "L0_conv_qkv_b", "L0_conv_proj_w",
        "L0_conv_proj_b"]


def kernel(**inputs):
    import numpy as np
    import concourse.bacc as bacc
    from concourse.bass_utils import run_bass_kernel_spmd

    nc = bacc.Bacc("TRN2", target_bir_lowering=False, num_devices=1)
    arrays, args = {}, []
    for name in _INS:
        a = np.ascontiguousarray(inputs[name])
        arrays[f"in_{name}"] = a
        args.append(nc.dram_tensor(f"in_{name}", a.shape, F32, kind="ExternalInput").ap())
    result = nc.dram_tensor("result", arrays["in_x"].shape, F32, kind="ExternalOutput").ap()
    attention_block(nc, *args, result)
    run = run_bass_kernel_spmd(nc, [arrays], core_ids=[0])
    return run.results[0]["result"]
```

```python
from contextlib import ExitStack

import concourse.bass as bass
from concourse import mybir

F32 = mybir.dt.float32
F32R = mybir.dt.float32r
ALU = mybir.AluOpType
ACT = mybir.ActivationFunctionType
AX = mybir.AxisListType

P = 128
BATCHES, TOKENS, C = 16, 1024, 512
BLOCKS = TOKENS // P
CH = 64
CHUNKS = C // CH
NPOS = P * CHUNKS
KT = C // P
GROUP = C // 32
EPS = 1e-6
SPB = BLOCKS * CHUNKS
N_SLOTS = BATCHES * SPB
N_BLOCKS = BATCHES * BLOCKS
N_HALVES = 2 * N_BLOCKS
N_PAIRS = N_BLOCKS // 2
PPB = BLOCKS // 2
XRING = 4

STAT_UNITS = {1: (0, 0, 4), 2: (1, 0, 2), 4: (1, 2, 4), 5: (2, 0, 2), 6: (2, 2, 4), 10: (3, 0, 2), 17: (3, 2, 4),
              18: (4, 0, 2), 20: (4, 2, 4), 21: (5, 0, 2), 22: (5, 2, 4), 26: (6, 0, 2), 33: (6, 2, 4),
              34: (7, 0, 2), 36: (7, 2, 4)}
STAT_SLOTS = list(STAT_UNITS)
AGGREGATE_SLOT = 36
GROUP_MEAN_SLOT = 37
GROUP_VAR_SLOT = 38
LARGE = -1


def within(n, count):
    return not isinstance(n, int) or 0 <= n < count


def before_start(b):
    return isinstance(b, int) and b == -1


def at_least(engine, sem, count):
    if not isinstance(count, int) or count > 0:
        engine.wait_ge(sem, count)


def large_unit(k):
    m = k % 16
    if m % 8 < 2:
        return "proj", 0, m % 8
    if m < 8:
        return "qk", m - 2, 0
    if m < 12:
        return "qk", m - 4, 0
    return "v", (m - 12) // 2, m % 2


def qk_column(n):
    return (n + KT) % (2 * KT)


def small_unit(k, place):
    m = k % 16
    if place != (0 if m in (1, 9, 13, 15) else 1):
        return ("spread", 0) if m == 15 else (None, 0)
    if m in (3, 7, 11):
        return "spread", 0
    if m in (9, 13):
        return "xt", (m - 9) // 4
    if k in STAT_SLOTS:
        return "stats", STAT_SLOTS.index(k)
    if k == GROUP_MEAN_SLOT:
        return "group", 0
    if k == GROUP_VAR_SLOT:
        return "group", 1
    return None, 0


def attention_block(nc, x, norm_scale, norm_bias, qkv_w, qkv_b, proj_w, proj_b, out):
    x_t = x.rearrange("b h w c -> b (h w) c").rearrange("b (n t) c -> b n t c", t=P)
    out_t = out.rearrange("b h w c -> b (h w) c").rearrange("b (n t) c -> b n t c", t=P)

    with ExitStack() as ctx:
        def sb(name, shape, dt=F32):
            return ctx.enter_context(nc.sbuf_tensor(name, shape, dt))

        def ps(name, shape):
            return ctx.enter_context(nc.psum_tensor(name, shape, F32))

        def sem(name):
            return ctx.enter_context(nc.semaphore(name))

        w_hi = sb("w_hi", [P, KT, 3 * C], F32R)
        w_lo = sb("w_lo", [P, KT, 3 * C], F32R)
        pw_hi = sb("pw_hi", [P, KT, C], F32R)
        pw_lo = sb("pw_lo", [P, KT, C], F32R)
        h_norm = sb("h_norm", [P, KT, 2 * P])
        h_hi = sb("h_hi", [P, KT, 2 * P], F32R)
        h_lo = sb("h_lo", [P, KT, 2 * P], F32R)
        x_pair = sb("x_pair", [P, XRING, 2, C])
        x_stat = sb("x_stat", [P, C])
        q_st = [[sb(f"q_{n}{g}", [P, 2, CHUNKS // 2, P], F32R) for n in "eo"] for g in range(2)]
        k_hi = [[sb(f"kh_{n}{g}", [P, 2, CHUNKS // 2, P], F32R) for n in "eo"] for g in range(2)]
        k_lo = [[sb(f"kl_{n}{g}", [P, 2, CHUNKS // 2, P], F32R) for n in "eo"] for g in range(2)]
        v_sb = [sb(f"v{g}", [P, 2, C]) for g in range(2)]
        probs = [sb(f"probs{i}", [P, NPOS]) for i in range(2)]
        probs_t = [sb(f"probs_t{i}", [P, CHUNKS, 4, P]) for i in range(2)]
        attn = sb("attn", [P, 2, 2 * P])
        attn_hi = sb("attn_hi", [P, 2, 2 * P], F32R)
        attn_lo = sb("attn_lo", [P, 2, 2 * P], F32R)
        inv_spread = sb("inv_spread", [P, 2 * P])
        v_bias = sb("v_bias", [P, C])
        p_bias = sb("p_bias", [P, C])
        ident = sb("ident", [P, P])
        group_avg = sb("group_avg", [P, P])
        qk_bias = sb("qk_bias", [P, 2 * KT])
        n_scale = sb("n_scale", [P, KT])
        n_bias = sb("n_bias", [P, KT])
        bn = sb("bn", [P, KT, BLOCKS, 6])
        mv = sb("mv", [P, KT, 2])
        gmv = sb("gmv", [P, KT, 2])
        dmean = sb("dmean", [P, KT])
        dsq = sb("dsq", [P, KT])
        gvar = sb("gvar", [P, KT])
        rstd = sb("rstd", [P, KT])
        mean_a = sb("mean_a", [P, KT])
        half_neg = sb("half_neg", [P, KT])
        x_mul = sb("x_mul", [P, KT])
        x_add = sb("x_add", [P, KT])
        neg_max = sb("neg_max", [P, 4])
        row_sum = [sb(f"row_sum{i}", [P, 4]) for i in range(2)]
        inv_sum = sb("inv_sum", [P, 4])
        inv_wide = sb("inv_wide", [P, 4, CH])

        w_stage = [probs_t[t // 2][:, 3 * (t % 2):3 * (t % 2) + 3, :, :].rearrange("p a b c -> p (a b c)")
                   for t in range(KT)]
        pw_stage = [probs[t // 2][:, (t % 2) * C:(t % 2 + 1) * C] for t in range(KT)]

        s_ps = [ps(f"s_ps{i}", [P, NPOS]) for i in range(2)]
        t_ps = [ps(f"t_ps{i}", [P, 4, P]) for i in range(2)]
        pv_ps = ps("pv_ps", [P, 2, 2 * P])
        c_ps = ps("c_ps", [P, C])

        w_loaded = [sem(f"w_loaded{i}") for i in range(KT)]
        pw_loaded = sem("pw_loaded")
        const_loaded = sem("const_loaded")
        const_made = sem("const_made")
        w_rounded = sem("w_rounded")
        w_ready = sem("w_ready")
        bias_scaled = sem("bias_scaled")
        pool_chain = sem("pool_chain")
        x_loaded = [sem(f"x_loaded{i}") for i in range(XRING)]
        stored = [sem(f"stored{i}") for i in range(XRING)]
        xs_loaded = sem("xs_loaded")
        stats_full = sem("stats_full")
        stats_taken = sem("stats_taken")
        aggregated = sem("aggregated")
        mean_off = sem("mean_off")
        group_full = sem("group_full")
        group_taken = sem("group_taken")
        affine_ready = sem("affine_ready")
        xt_full = sem("xt_full")
        xt_normed = sem("xt_normed")
        h_rounded = sem("h_rounded")
        h_split = sem("h_split")
        affine_step = sem("affine_step")
        residual_ready = sem("residual_ready")
        qk_full = sem("qk_full")
        qk_hi_done = sem("qk_hi_done")
        qk_ready = sem("qk_ready")
        k_doubled = sem("k_doubled")
        v_full = sem("v_full")
        v_ready = sem("v_ready")
        scores_full = sem("scores_full")
        max_ready = sem("max_ready")
        probs_ready = sem("probs_ready")
        t_full = [sem(f"t_full{i}") for i in range(2)]
        t_taken = [sem(f"t_taken{i}") for i in range(2)]
        pv_done = sem("pv_done")
        inv_ready = sem("inv_ready")
        inv_widened = sem("inv_widened")
        spread_full = sem("spread_full")
        spread_taken = sem("spread_taken")
        attn_ready = sem("attn_ready")
        attn_hi_done = sem("attn_hi_done")
        attn_lo_done = sem("attn_lo_done")
        proj_full = sem("proj_full")
        out_ready = sem("out_ready")

        def proj_block(b, k):
            return BLOCKS * b + k // 8 - 2

        def spread_half(b, k):
            return 2 * BLOCKS * b + k // 4 - 1

        def made_pair(b, k):
            return PPB * b + k // 16 + 1

        def xt_pair(b, k):
            return PPB * b + k // 16 + 2

        tenants = []
        for k in range(SPB):
            if large_unit(k)[2] == 0:
                tenants.append((k, LARGE))
            for place in range(2):
                if small_unit(k, place)[0]:
                    tenants.append((k, place))

        def stat_unit(b, k):
            u, first, end = STAT_UNITS[k]
            if before_start(b):
                return u, 0, KT if end == KT else 0, u + 1
            return u, first, end, BLOCKS + len(STAT_UNITS) * b + STAT_SLOTS.index(k) + 1

        def unit_bank(b, n):
            return s_ps[n % 2][:, 0:C] if before_start(b) else c_ps[:, :]

        def emptied(b, k, place):
            kind, n = large_unit(k)[:2] if place == LARGE else small_unit(k, place)
            if kind == "proj":
                h = proj_block(b, k)
                return within(h, N_BLOCKS), out_ready, h + 1
            if kind == "spread":
                half = spread_half(b, k)
                return within(half, N_HALVES), spread_taken, half + 1
            if kind == "qk":
                g = made_pair(b, k)
                return within(g, N_PAIRS), qk_ready, 2 * KT * g + n + 1
            if kind == "v":
                g = made_pair(b, k)
                return within(g, N_PAIRS), v_ready, 2 * g + n + 1
            if kind == "xt":
                g = xt_pair(b, k)
                return within(g, N_PAIRS), xt_normed, 2 * g + n + 1
            if kind == "stats":
                return within(b + 1, BATCHES) and stat_unit(b, k)[2] > 0, stats_taken, stat_unit(b, k)[3]
            return within(b + 1, BATCHES), group_taken, 2 * (b + 1) + n + 1

        def await_shared_bank(pe, b, k, place):
            i = tenants.index((k, place))
            for back in range(1, len(tenants) + 1):
                bb = b if i - back >= 0 else b - 1
                if isinstance(bb, int) and bb < -1:
                    return
                exists, taken, count = emptied(bb, *tenants[i - back])
                if exists:
                    pe.wait_ge(taken, count)
                    return

        def batches(engine, slot):
            for b in (-1, 0):
                for k in range(SPB):
                    slot(b, k)
            with engine.Fori(1, BATCHES - 1) as b:
                for k in range(SPB):
                    slot(b, k)
            for k in range(SPB):
                slot(BATCHES - 1, k)
            for k in range(18):
                slot(BATCHES, k)

        def copy_transposed(engine, copy, b, k, grp):
            n = (k - 1) // 4
            t = SPB * b + k - 1
            engine.wait_ge(t_full[grp], t + 1)
            if (k - 1) % 4 == 0:
                at_least(engine, pv_done, 2 * BLOCKS * b + n - 1)
            copy(probs_t[n % 2][:, 4 * grp:4 * grp + 4, (k - 1) % 4, :], t_ps[grp][:, :, :]).then_inc(t_taken[grp], 1)

        def at_least_aside(engine, sem, count):
            if isinstance(count, int):
                return at_least(engine, sem, count)
            engine.compute_val(count)
            engine.wait_ge(const_made, 2)
            engine.wait_ge(sem, count)

        block = ctx.enter_context(nc.Block())

        @block.sync
        def _(sp):
            for n in range(XRING):
                sp.dma_start(x_pair[:, n, :, :],
                             x_t[0, 2 * n:2 * n + 2].rearrange("n t c -> t n c")).then_inc(x_loaded[n], 16)

            def load_stat_tile(b, u, units):
                if within(b, BATCHES - 1):
                    at_least_aside(sp, stats_full, BLOCKS + len(STAT_UNITS) * b + units)
                    sp.dma_start(x_stat[:, :], x_t[b + 1, u]).then_inc(xs_loaded, 16)

            def slot(b, k):
                if k % 8 == 1:
                    h = proj_block(b, k)
                    n = (k - 1) // 8 - 2
                    if within(h, N_BLOCKS):
                        at_least_aside(sp, out_ready, h + 1)
                        ring = (n // 2) % XRING
                        sp.dma_start(out_t[b + n // BLOCKS, n % BLOCKS],
                                     x_pair[:, ring, n % 2, :]).then_inc(stored[ring], 16)
                if k % 16 == 2:
                    g = xt_pair(b, k)
                    n = k // 16 + 2
                    if within(g, N_PAIRS) and within(g - XRING, N_PAIRS):
                        at_least_aside(sp, stored[n % XRING], 32 * (b + n // PPB))
                        first = 2 * (n % PPB)
                        sp.dma_start(x_pair[:, n % XRING, :, :],
                                     x_t[b + n // PPB, first:first + 2].rearrange("n t c -> t n c")
                                     ).then_inc(x_loaded[n % XRING], 16)
                if k % 16 == 6:
                    g, buf = made_pair(b, k), (k // 16 + 1) % 2
                    if within(g, N_PAIRS):
                        at_least_aside(sp, qk_ready, 2 * KT * g + KT)
                        for pair in (k_hi[buf], k_lo[buf]):
                            sp.dma_start(pair[0][CH:P, :, :, :].bitcast(F32), pair[0][0:CH, :, :, :].bitcast(F32)).then_inc(k_doubled, 16)
                            sp.dma_start(pair[1][0:CH, :, :, :].bitcast(F32), pair[1][CH:P, :, :, :].bitcast(F32)).then_inc(k_doubled, 16)
                if k == 0:
                    load_stat_tile(b, 0, 0)
                if k in STAT_SLOTS[:-1] and STAT_UNITS[k][2] == KT:
                    load_stat_tile(b, STAT_UNITS[k][0] + 1, STAT_SLOTS.index(k) + 1)

            batches(sp, slot)
            for ring in range(XRING):
                sp.wait_ge(stored[ring], 16 * N_BLOCKS // XRING)

        @block.tensor
        def _(pe):
            def scores(b, k):
                s = SPB * b + k
                g, i, c, buf = PPB * b + k // 16, (k // 8) % 2, k % 8, (k // 16) % 2
                if k % 16 == 0:
                    pe.wait_ge(qk_ready, 2 * KT * (g + 1))
                    pe.wait_ge(k_doubled, 16 * 4 * (g + 1))
                if within(s - 2, N_SLOTS):
                    pe.wait_ge(probs_ready, s - 1)
                q = q_st[buf][c % 2][:, i, c // 2, :]
                for par in range(2):
                    dst = s_ps[k % 2][:, par * C:(par + 1) * C]
                    nc.tensor.matmul(dst, q, k_hi[buf][par][:, i, :, :].rearrange("p j t -> p (j t)"),
                                     start=True, stop=False)
                    last = nc.tensor.matmul(dst, q, k_lo[buf][par][:, i, :, :].rearrange("p j t -> p (j t)"),
                                            start=False, stop=True)
                last.then_inc(scores_full, 1)

            def transposes(b, k):
                t = SPB * b + k - 1
                pe.wait_ge(probs_ready, t + 1)
                for grp in range(2):
                    at_least(pe, t_taken[grp], t)
                    for n in range(4):
                        kt = 4 * grp + n
                        last = nc.tensor.transpose(t_ps[grp][:, n, :], probs[(k - 1) % 2][:, kt * P:(kt + 1) * P],
                                                   ident[:, :])
                    last.then_inc(t_full[grp], 1)

            def attend(b, k):
                n, part = (k - 5) // 4, (k - 5) % 4
                half = 2 * BLOCKS * b + n
                i, buf, side = (n // 2) % 2, (n // 4) % 2, n % 2
                if part == 0:
                    for grp in range(2):
                        pe.wait_ge(t_taken[grp], 4 * half + 4)
                    if n % 4 == 0:
                        pe.wait_ge(v_ready, 2 * (PPB * b + n // 4) + 2)
                    at_least(pe, attn_ready, half)
                for kt in (2 * part, 2 * part + 1):
                    chunk = 2 * (kt % 4) + kt // 4
                    for par in range(2):
                        last = nc.tensor.matmul(
                            pv_ps[CH * par:CH * (par + 1), side, :],
                            v_sb[buf][:, i, CH * chunk:CH * (chunk + 1)],
                            probs_t[side][:, kt, :, :].rearrange("p (a r) t -> p r a t", r=2)[:, par, :, :],
                            start=(kt == 0), stop=(kt == 7))
                if part == 3:
                    last.then_inc(pv_done, 1)

            def large(b, k):
                kind, n, part = large_unit(k)
                if kind == "proj":
                    h = proj_block(b, k)
                    if not within(h, N_BLOCKS):
                        return
                    if isinstance(h, int) and h == 0 and part == 0:
                        pe.wait_ge(w_ready, 2 * KT)
                    if part == 0:
                        pe.wait_ge(attn_lo_done, 2 * h + 2)
                        await_shared_bank(pe, b, k, LARGE)
                    for j in (2 * part, 2 * part + 1):
                        a_hi = attn_hi[:, j // 2, (j % 2) * P:(j % 2 + 1) * P]
                        a_lo = attn_lo[:, j // 2, (j % 2) * P:(j % 2 + 1) * P]
                        nc.tensor.matmul(c_ps[:, :], a_hi, pw_hi[:, j, :], start=(j == 0), stop=False)
                        nc.tensor.matmul(c_ps[:, :], a_hi, pw_lo[:, j, :], start=False, stop=False)
                        last = nc.tensor.matmul(c_ps[:, :], a_lo, pw_hi[:, j, :], start=False, stop=(j == 3))
                    if part == 1:
                        last.then_inc(proj_full, 1)
                    return
                g = made_pair(b, k)
                if not within(g, N_PAIRS):
                    return
                if kind == "qk":
                    if before_start(b) and n == 0:
                        pe.wait_ge(w_ready, KT)
                    if not before_start(b):
                        await_shared_bank(pe, b, k, LARGE)
                    elif n >= 2:
                        pe.wait_ge(qk_ready, n - 1)
                    bank, col = unit_bank(b, n), qk_column(n)
                    for t in range(KT):
                        if n == 0 and t % 2 == 0:
                            pe.wait_ge(h_split, 2 * g + t // 2 + 1)
                        wh, wl = (w[:, t, col * P:(col + 1) * P] for w in (w_hi, w_lo))
                        nc.tensor.matmul(bank[:, 0:2 * P], wh, h_hi[:, t, :], start=(t == 0), stop=False)
                        nc.tensor.matmul(bank[:, 0:2 * P], wh, h_lo[:, t, :], start=False, stop=False)
                        last = nc.tensor.matmul(bank[:, 0:2 * P], wl, h_hi[:, t, :], start=False, stop=(t == KT - 1))
                    last.then_inc(qk_full, 1)
                else:
                    if part == 0:
                        await_shared_bank(pe, b, k, LARGE)
                    for t in (2 * part, 2 * part + 1):
                        hh, hl = (h[:, t, n * P:(n + 1) * P] for h in (h_hi, h_lo))
                        nc.tensor.matmul(c_ps[:, :], hh, w_hi[:, t, 2 * C:3 * C], start=(t == 0), stop=False)
                        nc.tensor.matmul(c_ps[:, :], hh, w_lo[:, t, 2 * C:3 * C], start=False, stop=False)
                        last = nc.tensor.matmul(c_ps[:, :], hl, w_hi[:, t, 2 * C:3 * C], start=False, stop=(t == KT - 1))
                    if part == 1:
                        last.then_inc(v_full, 1)

            def small(b, k, place):
                kind, n = small_unit(k, place)
                if kind is None or not emptied(b, k, place)[0]:
                    return
                if kind == "stats":
                    u, first, end, _ = stat_unit(b, k)
                    if before_start(b):
                        pe.wait_ge(x_loaded[u // 2], 16)
                        if u >= 2:
                            pe.wait_ge(stats_taken, u - 1)
                        tile = x_pair[:, u // 2, u % 2, :]
                    else:
                        pe.wait_ge(xs_loaded, 16 * (BLOCKS * b + u + 1))
                        await_shared_bank(pe, b, k, place)
                        tile = x_stat[:, :]
                    bank = unit_bank(b, u)
                    for t in range(first, end):
                        last = nc.tensor.transpose(bank[:, t * P:(t + 1) * P], tile[:, t * P:(t + 1) * P], ident[:, :])
                    last.then_inc(stats_full, 1)
                elif kind == "group":
                    pe.wait_ge(aggregated, 2 * (b + 1) + n + 1)
                    await_shared_bank(pe, b, k, place)
                    src = mv[:, :, :].rearrange("p t s -> p (t s)") if n == 0 else dsq[:, :]
                    nc.tensor.matmul(c_ps[:, 0:(2 - n) * KT], group_avg[:, :], src,
                                     start=True, stop=True).then_inc(group_full, 1)
                elif kind == "xt":
                    ring = (k // 16 + 2) % XRING
                    if n == 0:
                        pe.wait_ge(x_loaded[ring], 16 * (b + (k // 16 + 2) // PPB + 1))
                    await_shared_bank(pe, b, k, place)
                    for t in range(2):
                        for i in range(2):
                            last = nc.tensor.transpose(c_ps[:, (2 * t + i) * P:(2 * t + i + 1) * P],
                                                       x_pair[:, ring, i, (2 * n + t) * P:(2 * n + t + 1) * P],
                                                       ident[:, :])
                    last.then_inc(xt_full, 1)
                else:
                    pe.wait_ge(inv_widened, spread_half(b, k) + 1)
                    await_shared_bank(pe, b, k, place)
                    for j in range(2):
                        inv = inv_wide[:, 2 * j:2 * j + 2, :].rearrange("p c n -> p (c n)")
                        last = nc.tensor.transpose(c_ps[:, j * P:(j + 1) * P], inv, ident[:, :])
                    last.then_inc(spread_full, 1)

            def slot(b, k):
                s = SPB * b + k
                if within(s, N_SLOTS):
                    scores(b, k)
                large(b, k)
                if within(s - 5, N_SLOTS):
                    attend(b, k)
                small(b, k, 0)
                if within(s - 1, N_SLOTS):
                    transposes(b, k)
                small(b, k, 1)

            pe.wait_ge(const_made, 2)
            batches(pe, slot)

        @block.scalar
        def _(act):
            def softmax_exp(b, k):
                s = SPB * b + k
                half, c = 2 * BLOCKS * b + k // 4, k % 4
                act.wait_ge(max_ready, s + 1)
                if within(s - 2, N_SLOTS):
                    act.wait_ge(t_full[1], s - 1)
                if c == 0 and within(half - 2, N_HALVES):
                    act.wait_ge(inv_ready, half - 1)
                nc.scalar.activation(probs[k % 2][:, :], s_ps[k % 2][:, :], ACT.Exp,
                                     bias=neg_max[:, k % 4:k % 4 + 1],
                                     accum_out=row_sum[(k // 4) % 2][:, c:c + 1]).then_inc(probs_ready, 1)

            def qk_hi(b, k, n):
                g, buf, j = made_pair(b, k), (k // 16 + 1) % 2, n % KT
                act.wait_ge(qk_full, 2 * KT * g + n + 1)
                if before_start(b) and n == 0:
                    act.wait_ge(bias_scaled, 1)
                if n == 0 and within(g - 2, N_PAIRS):
                    act.wait_ge(scores_full, 16 * (g - 1))
                low, high, bank = slice(0, CH), slice(CH, P), unit_bank(b, n)
                even, odd = k_hi[buf] if n < KT else q_st[buf]
                for dst, at in ((even, low), (odd, high)):
                    nc.scalar.activation(dst[at, :, j, :], bank[at, 0:2 * P].rearrange("p (i t) -> p i t", i=2),
                                         ACT.Identity, bias=qk_bias[at, qk_column(n):qk_column(n) + 1]
                                         ).then_inc(qk_hi_done, 1)

            def norm_x(b, k, n):
                g = xt_pair(b, k)
                act.wait_ge(xt_full, 2 * g + n + 1)
                if k == 2 * 16 + 9:
                    act.wait_ge(affine_ready, b + 2)
                if within(g - 1, N_PAIRS):
                    act.wait_ge(h_split, 2 * g)
                for t in range(2):
                    ct = 2 * n + t
                    last = nc.scalar.activation(h_norm[:, ct, :], c_ps[:, 2 * t * P:2 * (t + 1) * P], ACT.Identity,
                                                bias=x_add[:, ct:ct + 1], scale=x_mul[:, ct:ct + 1])
                last.then_inc(xt_normed, 1)

            def slot(b, k):
                s = SPB * b + k
                kind, n, _ = large_unit(k)
                if kind == "qk" and within(made_pair(b, k), N_PAIRS):
                    qk_hi(b, k, n)
                if within(s, N_SLOTS):
                    softmax_exp(b, k)
                if k % 4 == 1:
                    half, side = 2 * BLOCKS * b + k // 4 - 2, (k // 4) % 2
                    if within(half, N_HALVES):
                        act.wait_ge(attn_ready, half + 1)
                        at_least(act, proj_full, BLOCKS * b + k // 8 - 1)
                        nc.scalar.copy(attn_hi[:, side, :], attn[:, side, :]).then_inc(attn_hi_done, 1)
                kind, n = small_unit(k, 0)
                if kind == "xt" and within(xt_pair(b, k), N_PAIRS):
                    norm_x(b, k, n)
                if within(s - 1, N_SLOTS):
                    copy_transposed(act, nc.scalar.copy, b, k, 0)
                if small_unit(k, 1)[0] == "spread" and within(spread_half(b, k), N_HALVES):
                    half = spread_half(b, k)
                    act.wait_ge(spread_full, half + 1)
                    at_least(act, attn_ready, half)
                    nc.scalar.copy(inv_spread[:, :], c_ps[:, 0:2 * P]).then_inc(spread_taken, 1)

            for t in range(KT):
                act.dma_start(w_stage[t], qkv_w[t * P:(t + 1) * P, :]).then_inc(w_loaded[t], 16)
            for t in range(KT):
                act.dma_start(pw_stage[t], proj_w[t * P:(t + 1) * P, :]).then_inc(pw_loaded, 16)
            for t in range(KT):
                act.wait_ge(w_loaded[t], 16)
                for part in range(3):
                    cols = slice(part * C, (part + 1) * C)
                    nc.scalar.activation(w_hi[:, t, cols], w_stage[t][:, cols], ACT.Identity,
                                         scale=CH ** -0.5 if part == 1 else 1.0).then_inc(w_rounded, 1)
            act.wait_ge(pw_loaded, 16 * KT)
            for t in range(KT):
                nc.scalar.copy(pw_hi[:, t, :], pw_stage[t]).then_inc(w_rounded, 1)
            act.wait_ge(const_loaded, 16 * 5)
            batches(act, slot)

        @block.vector
        def _(dve):
            def split_qkv_weights(t):
                for part in range(3):
                    cols = slice(part * C, (part + 1) * C)
                    dve.wait_ge(w_rounded, 3 * t + part + 1)
                    last = nc.vector.scalar_tensor_tensor(
                        w_lo[:, t, cols], w_stage[t][:, cols], CH ** -0.5 if part == 1 else 1.0,
                        w_hi[:, t, cols].bitcast(F32), ALU.mult, ALU.subtract)
                last.then_inc(w_ready, 1)

            def split_proj_weights():
                for t in range(KT):
                    dve.wait_ge(w_rounded, 3 * KT + t + 1)
                    nc.vector.tensor_tensor(pw_lo[:, t, :], pw_stage[t], pw_hi[:, t, :].bitcast(F32),
                                            ALU.subtract).then_inc(w_ready, 1)
                dve.wait_ge(const_loaded, 16 * 5)
                nc.vector.tensor_scalar(qk_bias[:, KT:2 * KT], qk_bias[:, KT:2 * KT], CH ** -0.5, None,
                                        ALU.mult).then_inc(bias_scaled, 1)

            def qk_split(b, k, n):
                g, buf, j = made_pair(b, k), (k // 16 + 1) % 2, n % KT
                low, high, bank = slice(0, CH), slice(CH, P), unit_bank(b, n)
                if n >= KT:
                    places = ((q_st[buf][0], high, low, q_st[buf][0]), (q_st[buf][1], low, high, q_st[buf][1]))
                else:
                    places = ((k_lo[buf][0], low, low, k_hi[buf][0]), (k_lo[buf][1], high, high, k_hi[buf][1]))
                for half, (dst, to, of, hi) in enumerate(places):
                    dve.wait_ge(qk_hi_done, 2 * (2 * KT * g + n) + half + 1)
                    last = nc.vector.scalar_tensor_tensor(
                        dst[to, :, j, :], bank[of, 0:2 * P].rearrange("p (i t) -> p i t", i=2), qk_bias[of, qk_column(n):qk_column(n) + 1],
                        hi[of, :, j, :].bitcast(F32), ALU.add, ALU.subtract)
                last.then_inc(qk_ready, 1)

            def slot(b, k):
                s = SPB * b + k
                if within(s, N_SLOTS):
                    dve.wait_ge(scores_full, s + 1)
                    nc.vector.tensor_reduce(neg_max[:, k % 4:k % 4 + 1], s_ps[k % 2][:, :], AX.X, ALU.max,
                                            negate=True).then_inc(max_ready, 1)
                if k % 4 == 0:
                    half = 2 * BLOCKS * b + k // 4 - 1
                    if within(half, N_HALVES):
                        dve.wait_ge(probs_ready, 4 * half + 4)
                        at_least(dve, inv_widened, half)
                        nc.vector.reciprocal(inv_sum[:, :], row_sum[(k // 4 - 1) % 2][:, :]).then_inc(inv_ready, 1)
                kind, n, part = large_unit(k)
                if kind == "qk" and within(made_pair(b, k), N_PAIRS):
                    qk_split(b, k, n)
                if kind == "v" and part == 1 and within(made_pair(b, k), N_PAIRS):
                    g = made_pair(b, k)
                    dve.wait_ge(v_full, 2 * g + n + 1)
                    if n == 0 and within(g - 2, N_PAIRS):
                        dve.wait_ge(pv_done, 4 * (g - 1))
                    nc.vector.tensor_tensor(v_sb[(k // 16 + 1) % 2][:, n, :], c_ps[:, :], v_bias[:, :],
                                            ALU.add).then_inc(v_ready, 1)
                if kind == "proj" and part == 1:
                    h, n = proj_block(b, k), k // 8 - 2
                    if within(h, N_BLOCKS):
                        dve.wait_ge(proj_full, h + 1)
                        if n % 2 == 0:
                            dve.wait_ge(residual_ready, PPB * b + n // 2 + 1)
                        r = x_pair[:, (n // 2) % XRING, n % 2, :]
                        nc.vector.tensor_tensor(r, c_ps[:, :], r, ALU.add).then_inc(out_ready, 1)
                if k % 4 == 0:
                    half, side = 2 * BLOCKS * b + k // 4 - 2, (k // 4) % 2
                    if within(half, N_HALVES):
                        dve.wait_ge(pv_done, half + 1)
                        dve.wait_ge(spread_taken, half + 1)
                        at_least(dve, attn_lo_done, half - 1)
                        nc.vector.tensor_tensor(attn[:, side, :], pv_ps[:, side, :], inv_spread[:, :],
                                                ALU.mult).then_inc(attn_ready, 1)
                statistics(b, k)
                if before_start(b) and k in STAT_UNITS and STAT_UNITS[k][2] == KT and STAT_UNITS[k][0] % 2:
                    split_qkv_weights(STAT_UNITS[k][0] // 2)
                if before_start(b) and k == GROUP_VAR_SLOT:
                    split_proj_weights()
                if within(s - 1, N_SLOTS):
                    copy_transposed(dve, nc.vector.tensor_copy, b, k, 1)

            def statistics(b, k):
                if not within(b + 1, BATCHES):
                    return
                nb = b + 1
                if k in STAT_SLOTS and stat_unit(b, k)[2] > 0:
                    u, first, end, units = stat_unit(b, k)
                    bank = unit_bank(b, u)
                    dve.wait_ge(stats_full, units)
                    if k == STAT_SLOTS[0]:
                        at_least(dve, aggregated, 2 * nb)
                    for t in range(first, end):
                        last = nc.vector.bn_stats(bn[:, t, u, :], bank[:, t * P:(t + 1) * P])
                    last.then_inc(stats_taken, 1)
                if k == AGGREGATE_SLOT:
                    at_least_aside(dve, stats_taken, stat_unit(b, k)[3])
                    for t in range(KT):
                        last = nc.vector.bn_aggr(mv[:, t, :], bn[:, t, :, :].rearrange("p u s -> p (u s)"))
                    last.then_inc(aggregated, 1)
                if k == GROUP_MEAN_SLOT:
                    dve.wait_ge(group_full, 2 * nb + 1)
                    at_least(dve, affine_ready, nb)
                    nc.vector.tensor_copy(gmv[:, :, :].rearrange("p t s -> p (t s)"), c_ps[:, 0:2 * KT]).then_inc(group_taken, 1)
                    dve.wait_ge(group_taken, 2 * nb + 1)
                    nc.vector.tensor_tensor(dmean[:, :], mv[:, :, 0], gmv[:, :, 0], ALU.subtract).then_inc(mean_off, 1)
                    dve.wait_ge(mean_off, nb + 1)
                    nc.vector.tensor_tensor(dsq[:, :], dmean[:, :], dmean[:, :], ALU.mult).then_inc(aggregated, 1)
                if k == GROUP_VAR_SLOT:
                    dve.wait_ge(group_full, 2 * nb + 2)
                    nc.vector.scalar_tensor_tensor(gvar[:, :], c_ps[:, 0:KT], EPS, gmv[:, :, 1],
                                                   ALU.add, ALU.add).then_inc(group_taken, 1)

            batches(dve, slot)

        @block.gpsimd
        def _(pool):
            def broadcast_row(row):
                return row.rearrange("(a n) -> a n", a=1).broadcast_to([P, C])

            pool.dma_start(v_bias[:, :], broadcast_row(qkv_b[2 * C:3 * C])).then_inc(const_loaded, 16)
            pool.dma_start(p_bias[:, :], broadcast_row(proj_b)).then_inc(const_loaded, 16)
            with nc.allow_non_contiguous_dma("vectors to the partitions, once"):
                pool.dma_start(qk_bias[:, :], qkv_b[0:2 * C].rearrange("(j p) -> p j", p=P)).then_inc(const_loaded, 16)
                pool.dma_start(n_scale[:, :], norm_scale.rearrange("(j p) -> p j", p=P)).then_inc(const_loaded, 16)
                pool.dma_start(n_bias[:, :], norm_bias.rearrange("(j p) -> p j", p=P)).then_inc(const_loaded, 16)
            nc.gpsimd.memset(ident[:, :], 0.0).then_inc(pool_chain, 1)
            nc.gpsimd.memset(group_avg[:, :], 1.0 / GROUP).then_inc(pool_chain, 1)
            nc.gpsimd.memset(half_neg[:, :], -0.5).then_inc(pool_chain, 1)
            pool.wait_ge(pool_chain, 3)
            nc.gpsimd.affine_select(out=ident[:, :], in_=ident[:, :], compare_op=ALU.not_equal, fill=1.0, base=0,
                                    pattern=[[-1, P]], channel_multiplier=1).then_inc(const_made, 1)
            groups = group_avg[:, :].rearrange("p (g c) -> p g c", c=GROUP)
            nc.gpsimd.affine_select(out=groups, in_=groups, compare_op=ALU.is_ge, fill=0.0, base=0,
                                    pattern=[[-GROUP, P // GROUP], [0, GROUP]], channel_multiplier=1).then_inc(pool_chain, 1)
            pool.wait_ge(pool_chain, 4)
            nc.gpsimd.affine_select(out=groups, in_=groups, compare_op=ALU.is_ge, fill=0.0, base=GROUP - 1,
                                    pattern=[[GROUP, P // GROUP], [0, GROUP]], channel_multiplier=-1).then_inc(const_made, 1)
            pool.wait_ge(const_loaded, 16 * 5)

            def split_h(b, k):
                g = xt_pair(b, k)
                at_least_aside(pool, v_full, 2 * g)
                for n in range(2):
                    part = slice(2 * n, 2 * n + 2)
                    at_least_aside(pool, xt_normed, 2 * g + n + 1)
                    nc.gpsimd.tensor_copy(h_hi[:, part, :], h_norm[:, part, :]).then_inc(h_rounded, 1)
                    pool.wait_ge(h_rounded, 2 * g + n + 1)
                    nc.gpsimd.tensor_tensor(h_lo[:, part, :], h_norm[:, part, :], h_hi[:, part, :].bitcast(F32),
                                            ALU.subtract).then_inc(h_split, 1)

            def affine(b):
                nb = b + 1
                pool.wait_ge(group_taken, 2 * nb + 2)
                nc.gpsimd.tensor_tensor(rstd[:, :], gvar[:, :], half_neg[:, :], ALU.pow).then_inc(affine_step, 1)
                at_least(pool, xt_normed, 2 * PPB * nb)
                pool.wait_ge(affine_step, 3 * nb + 1)
                nc.gpsimd.tensor_tensor(x_mul[:, :], rstd[:, :], n_scale[:, :], ALU.mult).then_inc(affine_step, 1)
                pool.wait_ge(affine_step, 3 * nb + 2)
                nc.gpsimd.tensor_tensor(mean_a[:, :], gmv[:, :, 0], x_mul[:, :], ALU.mult).then_inc(affine_step, 1)
                pool.wait_ge(affine_step, 3 * nb + 3)
                nc.gpsimd.tensor_tensor(x_add[:, :], n_bias[:, :], mean_a[:, :], ALU.subtract).then_inc(affine_ready, 1)

            def slot(b, k):
                if k % 16 == 15 and within(xt_pair(b, k), N_PAIRS):
                    split_h(b, k)
                if k % 16 == 1:
                    g, n = made_pair(b, k), k // 16 + 1
                    if within(g, N_PAIRS):
                        pool.wait_ge(xt_full, 2 * g + 2)
                        for i in range(2):
                            r = x_pair[:, n % XRING, i, :]
                            last = nc.gpsimd.tensor_tensor(r, r, p_bias[:, :], ALU.add)
                        last.then_inc(residual_ready, 1)
                if k % 4 == 0:
                    half = 2 * BLOCKS * b + k // 4 - 1
                    if within(half, N_HALVES):
                        at_least_aside(pool, spread_full, half)
                        at_least_aside(pool, inv_ready, half + 1)
                        nc.gpsimd.tensor_copy(inv_wide[:, :, :], inv_sum[:, :].unsqueeze(2).broadcast_to([P, 4, CH])
                                              ).then_inc(inv_widened, 1)
                if k % 4 == 1:
                    half, side = 2 * BLOCKS * b + k // 4 - 2, (k // 4) % 2
                    if within(half, N_HALVES):
                        pool.wait_ge(attn_hi_done, half + 1)
                        at_least(pool, proj_full, BLOCKS * b + k // 8 - 1)
                        nc.gpsimd.tensor_tensor(attn_lo[:, side, :], attn[:, side, :], attn_hi[:, side, :].bitcast(F32),
                                                ALU.subtract).then_inc(attn_lo_done, 1)
                if k == GROUP_VAR_SLOT and within(b + 1, BATCHES):
                    affine(b)

            batches(pool, slot)


_INS = ["x", "L0_conv_norm_scale", "L0_conv_norm_bias", "L0_conv_qkv_w", "L0_conv_qkv_b", "L0_conv_proj_w",
        "L0_conv_proj_b"]


def kernel(**inputs):
    import numpy as np
    import concourse.bacc as bacc
    from concourse.bass_utils import run_bass_kernel_spmd

    nc = bacc.Bacc("TRN2", target_bir_lowering=False, num_devices=1)
    arrays, args = {}, []
    for name in _INS:
        a = np.ascontiguousarray(inputs[name])
        arrays[f"in_{name}"] = a
        args.append(nc.dram_tensor(f"in_{name}", a.shape, F32, kind="ExternalInput").ap())
    result = nc.dram_tensor("result", arrays["in_x"].shape, F32, kind="ExternalOutput").ap()
    attention_block(nc, *args, result)
    run = run_bass_kernel_spmd(nc, [arrays], core_ids=[0])
    return run.results[0]["result"]
```

```python
from contextlib import ExitStack

import concourse.bass as bass
from concourse import mybir

F32 = mybir.dt.float32
F32R = mybir.dt.float32r
ALU = mybir.AluOpType
ACT = mybir.ActivationFunctionType
AX = mybir.AxisListType

P = 128
BATCHES, TOKENS, C = 16, 1024, 512
BLOCKS = TOKENS // P
CH = 64
CHUNKS = C // CH
NPOS = P * CHUNKS
KT = C // P
GROUP = C // 32
EPS = 1e-6
SPB = BLOCKS * CHUNKS
N_SLOTS = BATCHES * SPB
N_BLOCKS = BATCHES * BLOCKS
N_HALVES = 2 * N_BLOCKS
N_PAIRS = N_BLOCKS // 2
PPB = BLOCKS // 2
XRING = 2

STAT_SLOTS = [1, 9, 13, 15, 17, 25, 33, 38]
AGGREGATE_SLOT = 39
GROUP_MEAN_SLOT = 42
GROUP_VAR_SLOT = 43
LARGE = -1


def within(n, count):
    return not isinstance(n, int) or 0 <= n < count


def before_start(b):
    return isinstance(b, int) and b == -1


def at_least(engine, sem, count):
    if not isinstance(count, int) or count > 0:
        engine.wait_ge(sem, count)


def large_unit(k):
    m = k % 16
    if m % 8 < 2:
        return "proj", 0, m % 8
    if m < 8:
        return "qk", m - 2, 0
    if m < 12:
        return "qk", m - 4, 0
    return "v", (m - 12) // 2, m % 2


def qk_column(n):
    return (n + KT) % (2 * KT)


def small_unit(k, place):
    m = k % 16
    if place != (0 if m in (1, 9, 13, 15) else 1):
        return None, 0
    if k in STAT_SLOTS:
        return "stats", STAT_SLOTS.index(k)
    if k == GROUP_MEAN_SLOT:
        return "group", 0
    if k == GROUP_VAR_SLOT:
        return "group", 1
    return None, 0


def attention_block(nc, x, norm_scale, norm_bias, qkv_w, qkv_b, proj_w, proj_b, out):
    x_t = x.rearrange("b h w c -> b (h w) c").rearrange("b (n t) c -> b n t c", t=P)
    out_t = out.rearrange("b h w c -> b (h w) c").rearrange("b (n t) c -> b n t c", t=P)

    with ExitStack() as ctx:
        def sb(name, shape, dt=F32):
            return ctx.enter_context(nc.sbuf_tensor(name, shape, dt))

        def ps(name, shape):
            return ctx.enter_context(nc.psum_tensor(name, shape, F32))

        def sem(name):
            return ctx.enter_context(nc.semaphore(name))

        w_hi = sb("w_hi", [P, KT, 3 * C], F32R)
        w_lo = sb("w_lo", [P, KT, 3 * C], F32R)
        pw_hi = sb("pw_hi", [P, KT, C], F32R)
        pw_lo = sb("pw_lo", [P, KT, C], F32R)
        xt_sb = sb("xt_sb", [P, PPB, KT, 2 * P])
        h_hi = sb("h_hi", [P, KT, 2 * P], F32R)
        h_lo = sb("h_lo", [P, KT, 2 * P], F32R)
        x_pair = sb("x_pair", [P, XRING, 2, C])
        x_next = sb("x_next", [P, C])
        q_st = [[sb(f"q_{n}{g}", [P, 2, CHUNKS // 2, P], F32R) for n in "eo"] for g in range(2)]
        k_hi = [[sb(f"kh_{n}{g}", [P, 2, CHUNKS // 2, P], F32R) for n in "eo"] for g in range(2)]
        k_lo = [[sb(f"kl_{n}{g}", [P, 2, CHUNKS // 2, P], F32R) for n in "eo"] for g in range(2)]
        v_sb = [sb(f"v{g}", [P, 2, C]) for g in range(2)]
        probs = [sb(f"probs{i}", [P, NPOS]) for i in range(2)]
        probs_t = [sb(f"probs_t{i}", [P, CHUNKS, 4, P]) for i in range(2)]
        attn_hi = sb("attn_hi", [P, 3, 2 * P], F32R)
        attn_lo = sb("attn_lo", [P, 3, 2 * P], F32R)
        v_bias = sb("v_bias", [P, C])
        p_bias = sb("p_bias", [P, C])
        ident = sb("ident", [P, P])
        group_avg = sb("group_avg", [P, P])
        qk_bias = sb("qk_bias", [P, 2 * KT])
        n_scale = sb("n_scale", [P, KT])
        n_bias = sb("n_bias", [P, KT])
        bn = sb("bn", [P, KT, BLOCKS, 6])
        mv = sb("mv", [P, KT, 2])
        gmv = sb("gmv", [P, KT, 2])
        dmean = sb("dmean", [P, KT])
        dsq = sb("dsq", [P, KT])
        gvar = sb("gvar", [P, KT])
        rstd = sb("rstd", [P, KT])
        mean_a = sb("mean_a", [P, KT])
        half_neg = sb("half_neg", [P, KT])
        x_mul = sb("x_mul", [P, KT])
        x_add = sb("x_add", [P, KT])
        neg_max = sb("neg_max", [P, 4])
        row_sum = sb("row_sum", [P, 2])
        inv_sum = sb("inv_sum", [P, 1])

        w_stage = [probs_t[t // 2][:, 3 * (t % 2):3 * (t % 2) + 3, :, :].rearrange("p a b c -> p (a b c)")
                   for t in range(KT)]
        pw_stage = [probs[t // 2][:, (t % 2) * C:(t % 2 + 1) * C] for t in range(KT)]

        x_start = [x_pair[:, 0, :, :], x_pair[:, 1, :, :], v_sb[0][:, :, :], v_sb[1][:, :, :]]

        s_ps = [ps(f"s_ps{i}", [P, NPOS]) for i in range(2)]
        t_ps = ps("t_ps", [P, CHUNKS, P])
        pv_ps = ps("pv_ps", [P, 2, 2 * P])
        c_ps = ps("c_ps", [P, C])

        w_loaded = [sem(f"w_loaded{i}") for i in range(KT)]
        pw_loaded = sem("pw_loaded")
        const_loaded = sem("const_loaded")
        const_made = sem("const_made")
        w_rounded = sem("w_rounded")
        w_ready = sem("w_ready")
        bias_scaled = sem("bias_scaled")
        pool_chain = sem("pool_chain")
        x_loaded = [sem(f"x_loaded{i}") for i in range(XRING)]
        stored = [sem(f"stored{i}") for i in range(XRING)]
        x_start_loaded = [sem(f"x_start_loaded{i}") for i in range(PPB)]
        xs_loaded = sem("xs_loaded")
        xt_full = sem("xt_full")
        xt_copied = sem("xt_copied")
        bn_done = sem("bn_done")
        aggregated = sem("aggregated")
        mean_off = sem("mean_off")
        group_full = sem("group_full")
        group_taken = sem("group_taken")
        affine_ready = sem("affine_ready")
        xt_normed = sem("xt_normed")
        h_rounded = sem("h_rounded")
        h_split = sem("h_split")
        affine_step = sem("affine_step")
        residual_ready = sem("residual_ready")
        qk_full = sem("qk_full")
        qk_hi_done = sem("qk_hi_done")
        qk_ready = sem("qk_ready")
        k_doubled = sem("k_doubled")
        v_full = sem("v_full")
        v_ready = sem("v_ready")
        scores_full = sem("scores_full")
        max_ready = sem("max_ready")
        probs_ready = sem("probs_ready")
        t_full = sem("t_full")
        t_taken = sem("t_taken")
        pv_done = sem("pv_done")
        inv_ready = sem("inv_ready")
        probs_scaled = sem("probs_scaled")
        attn_hi_done = sem("attn_hi_done")
        attn_ready = sem("attn_ready")
        proj_full = sem("proj_full")
        out_ready = sem("out_ready")

        def proj_block(b, k):
            return BLOCKS * b + k // 8 - 2

        def attended_pair(b, k):
            return PPB * b + k // 16

        def made_pair(b, k):
            return PPB * b + k // 16 + 1

        def xt_pair(b, k):
            return PPB * b + k // 16 + 2

        tenants = []
        for k in range(SPB):
            if large_unit(k)[2] == 0:
                tenants.append((k, LARGE))
            for place in range(2):
                if small_unit(k, place)[0]:
                    tenants.append((k, place))

        def attn_place(h, side):
            return 2 if side else h % 2

        def unit_bank(b, n):
            return s_ps[n % 2][:, 0:C] if before_start(b) else c_ps[:, :]

        def emptied(b, k, place):
            kind, n = large_unit(k)[:2] if place == LARGE else small_unit(k, place)
            if kind == "proj":
                h = proj_block(b, k)
                return within(h, N_BLOCKS), out_ready, h + 1
            if kind == "qk":
                g = made_pair(b, k)
                return within(g, N_PAIRS), qk_ready, 2 * KT * g + n + 1
            if kind == "v":
                g = made_pair(b, k)
                return within(g, N_PAIRS), v_ready, 2 * g + n + 1
            if kind == "stats":
                return within(b + 1, BATCHES), xt_copied, BLOCKS * (b + 1) + n + 1
            return within(b + 1, BATCHES), group_taken, 2 * (b + 1) + n + 1

        def await_shared_bank(pe, b, k, place):
            i = tenants.index((k, place))
            for back in range(1, len(tenants) + 1):
                bb = b if i - back >= 0 else b - 1
                if isinstance(bb, int) and bb < -1:
                    return
                exists, taken, count = emptied(bb, *tenants[i - back])
                if exists:
                    pe.wait_ge(taken, count)
                    return

        def batches(engine, slot):
            for b in (-1, 0):
                for k in range(SPB):
                    slot(b, k)
            with engine.Fori(1, BATCHES - 1) as b:
                for k in range(SPB):
                    slot(b, k)
            for k in range(SPB):
                slot(BATCHES - 1, k)
            for k in range(10):
                slot(BATCHES, k)

        def at_least_aside(engine, sem, count):
            if isinstance(count, int):
                return at_least(engine, sem, count)
            engine.compute_val(count)
            engine.wait_ge(const_made, 2)
            engine.wait_ge(sem, count)

        block = ctx.enter_context(nc.Block())

        @block.sync
        def _(sp):
            for n in range(PPB):
                sp.dma_start(x_start[n], x_t[0, 2 * n:2 * n + 2].rearrange("n t c -> t n c")
                             ).then_inc(x_start_loaded[n], 16)

            def load_x_tile(b, u):
                if within(b, BATCHES - 1):
                    at_least_aside(sp, xt_full, BLOCKS * (b + 1) + u)
                    sp.dma_start(x_next[:, :], x_t[b + 1, u]).then_inc(xs_loaded, 16)

            def slot(b, k):
                if k % 8 == 1:
                    h = proj_block(b, k)
                    n = (k - 1) // 8 - 2
                    if within(h, N_BLOCKS):
                        at_least_aside(sp, out_ready, h + 1)
                        ring = (n // 2) % XRING
                        sp.dma_start(out_t[b + n // BLOCKS, n % BLOCKS],
                                     x_pair[:, ring, n % 2, :]).then_inc(stored[ring], 16)
                if k % 16 == 2:
                    g, n = attended_pair(b, k), k // 16
                    if within(g, N_PAIRS):
                        at_least_aside(sp, stored[n % XRING], 32 * (PPB // XRING * b + n // XRING))
                        first = 2 * n
                        sp.dma_start(x_pair[:, n % XRING, :, :],
                                     x_t[b, first:first + 2].rearrange("n t c -> t n c")
                                     ).then_inc(x_loaded[n % XRING], 16)
                if k % 16 == 6:
                    g, buf = made_pair(b, k), (k // 16 + 1) % 2
                    if within(g, N_PAIRS):
                        at_least_aside(sp, qk_ready, 2 * KT * g + KT)
                        for pair in (k_hi[buf], k_lo[buf]):
                            even, odd = (half[:, :, :, :].bitcast(F32) for half in pair)
                            sp.dma_start(even[CH:P], even[0:CH]).then_inc(k_doubled, 16)
                            sp.dma_start(odd[0:CH], odd[CH:P]).then_inc(k_doubled, 16)
                if k == 0:
                    load_x_tile(b, 0)
                if k in STAT_SLOTS[:-1]:
                    load_x_tile(b, STAT_SLOTS.index(k) + 1)

            batches(sp, slot)
            for ring in range(XRING):
                sp.wait_ge(stored[ring], 16 * N_BLOCKS // XRING)

        @block.tensor
        def _(pe):
            def scores(b, k):
                s = SPB * b + k
                g, i, c, buf = PPB * b + k // 16, (k // 8) % 2, k % 8, (k // 16) % 2
                if k % 16 == 0:
                    pe.wait_ge(qk_ready, 2 * KT * (g + 1))
                    pe.wait_ge(k_doubled, 16 * 4 * (g + 1))
                if within(s - 2, N_SLOTS):
                    pe.wait_ge(probs_ready, s - 1)
                q = q_st[buf][c % 2][:, i, c // 2, :]
                for par in range(2):
                    dst = s_ps[k % 2][:, par * C:(par + 1) * C]
                    nc.tensor.matmul(dst, q, k_hi[buf][par][:, i, :, :].rearrange("p j t -> p (j t)"),
                                     start=True, stop=False)
                    last = nc.tensor.matmul(dst, q, k_lo[buf][par][:, i, :, :].rearrange("p j t -> p (j t)"),
                                            start=False, stop=True)
                last.then_inc(scores_full, 1)

            def transposes(b, k):
                t = SPB * b + k - 1
                pe.wait_ge(probs_scaled, t + 1)
                at_least(pe, t_taken, t)
                for kt in range(CHUNKS):
                    last = nc.tensor.transpose(t_ps[:, kt, :], probs[(k - 1) % 2][:, kt * P:(kt + 1) * P],
                                               ident[:, :])
                last.then_inc(t_full, 1)

            def attend(b, k):
                n, part = (k - 5) // 4, (k - 5) % 4
                half = 2 * BLOCKS * b + n
                i, buf, side = (n // 2) % 2, (n // 4) % 2, n % 2
                if part == 0:
                    pe.wait_ge(t_taken, 4 * half + 4)
                    if n % 4 == 0:
                        pe.wait_ge(v_ready, 2 * (PPB * b + n // 4) + 2)
                    at_least(pe, attn_ready, half)
                for kt in (2 * part, 2 * part + 1):
                    chunk = 2 * (kt % 4) + kt // 4
                    for par in range(2):
                        last = nc.tensor.matmul(
                            pv_ps[CH * par:CH * (par + 1), side, :],
                            v_sb[buf][:, i, CH * chunk:CH * (chunk + 1)],
                            probs_t[side][:, kt, :, :].rearrange("p (a r) t -> p r a t", r=2)[:, par, :, :],
                            start=(kt == 0), stop=(kt == 7))
                if part == 3:
                    last.then_inc(pv_done, 1)

            def large(b, k):
                kind, n, part = large_unit(k)
                if kind == "proj":
                    h = proj_block(b, k)
                    if not within(h, N_BLOCKS):
                        return
                    if isinstance(h, int) and h == 0 and part == 0:
                        pe.wait_ge(w_ready, 2 * KT)
                    if part == 0:
                        pe.wait_ge(attn_ready, 2 * h + 2)
                        await_shared_bank(pe, b, k, LARGE)
                    for j in (2 * part, 2 * part + 1):
                        a_hi = attn_hi[:, attn_place(k // 8, j // 2), (j % 2) * P:(j % 2 + 1) * P]
                        a_lo = attn_lo[:, attn_place(k // 8, j // 2), (j % 2) * P:(j % 2 + 1) * P]
                        nc.tensor.matmul(c_ps[:, :], a_hi, pw_hi[:, j, :], start=(j == 0), stop=False)
                        nc.tensor.matmul(c_ps[:, :], a_hi, pw_lo[:, j, :], start=False, stop=False)
                        last = nc.tensor.matmul(c_ps[:, :], a_lo, pw_hi[:, j, :], start=False, stop=(j == 3))
                    if part == 1:
                        last.then_inc(proj_full, 1)
                    return
                g = made_pair(b, k)
                if not within(g, N_PAIRS):
                    return
                if kind == "qk":
                    if before_start(b) and n == 0:
                        pe.wait_ge(w_ready, KT)
                    if not before_start(b):
                        await_shared_bank(pe, b, k, LARGE)
                    elif n >= 2:
                        pe.wait_ge(qk_ready, n - 1)
                    bank, col = unit_bank(b, n), qk_column(n)
                    for t in range(KT):
                        if n == 0 and t % 2 == 0:
                            pe.wait_ge(h_split, 2 * g + t // 2 + 1)
                        wh, wl = (w[:, t, col * P:(col + 1) * P] for w in (w_hi, w_lo))
                        nc.tensor.matmul(bank[:, 0:2 * P], wh, h_hi[:, t, :], start=(t == 0), stop=False)
                        nc.tensor.matmul(bank[:, 0:2 * P], wh, h_lo[:, t, :], start=False, stop=False)
                        last = nc.tensor.matmul(bank[:, 0:2 * P], wl, h_hi[:, t, :], start=False, stop=(t == KT - 1))
                    last.then_inc(qk_full, 1)
                else:
                    if part == 0:
                        await_shared_bank(pe, b, k, LARGE)
                    for t in (2 * part, 2 * part + 1):
                        hh, hl = (h[:, t, n * P:(n + 1) * P] for h in (h_hi, h_lo))
                        nc.tensor.matmul(c_ps[:, :], hh, w_hi[:, t, 2 * C:3 * C], start=(t == 0), stop=False)
                        nc.tensor.matmul(c_ps[:, :], hh, w_lo[:, t, 2 * C:3 * C], start=False, stop=False)
                        last = nc.tensor.matmul(c_ps[:, :], hl, w_hi[:, t, 2 * C:3 * C], start=False, stop=(t == KT - 1))
                    if part == 1:
                        last.then_inc(v_full, 1)

            def small(b, k, place):
                kind, n = small_unit(k, place)
                if kind is None or not emptied(b, k, place)[0]:
                    return
                if kind == "stats":
                    if before_start(b):
                        pe.wait_ge(x_start_loaded[n // 2], 16)
                        if n >= 2:
                            pe.wait_ge(xt_copied, n - 1)
                        tile = x_start[n // 2][:, n % 2, :]
                    else:
                        pe.wait_ge(xs_loaded, 16 * (BLOCKS * b + n + 1))
                        await_shared_bank(pe, b, k, place)
                        tile = x_next[:, :]
                    bank = unit_bank(b, n)
                    for t in range(KT):
                        last = nc.tensor.transpose(bank[:, t * P:(t + 1) * P], tile[:, t * P:(t + 1) * P], ident[:, :])
                    last.then_inc(xt_full, 1)
                elif kind == "group":
                    pe.wait_ge(aggregated, 2 * (b + 1) + n + 1)
                    await_shared_bank(pe, b, k, place)
                    src = mv[:, :, :].rearrange("p t s -> p (t s)") if n == 0 else dsq[:, :]
                    nc.tensor.matmul(c_ps[:, 0:(2 - n) * KT], group_avg[:, :], src,
                                     start=True, stop=True).then_inc(group_full, 1)

            def slot(b, k):
                s = SPB * b + k
                if within(s, N_SLOTS):
                    scores(b, k)
                large(b, k)
                if within(s - 5, N_SLOTS):
                    attend(b, k)
                small(b, k, 0)
                if within(s - 1, N_SLOTS):
                    transposes(b, k)
                small(b, k, 1)

            pe.wait_ge(const_made, 2)
            batches(pe, slot)

        @block.scalar
        def _(act):
            def softmax_exp(b, k):
                s = SPB * b + k
                act.wait_ge(max_ready, s + 1)
                if within(s - 2, N_SLOTS):
                    act.wait_ge(t_full, s - 1)
                nc.scalar.activation(probs[k % 2][:, :], s_ps[k % 2][:, :], ACT.Exp,
                                     bias=neg_max[:, k % 4:k % 4 + 1],
                                     accum_out=row_sum[:, k % 2:k % 2 + 1]).then_inc(probs_ready, 1)

            def qk_hi(b, k, n):
                g, buf, j = made_pair(b, k), (k // 16 + 1) % 2, n % KT
                act.wait_ge(qk_full, 2 * KT * g + n + 1)
                if before_start(b) and n == 0:
                    act.wait_ge(bias_scaled, 1)
                if n == 0 and within(g - 2, N_PAIRS):
                    act.wait_ge(scores_full, 16 * (g - 1))
                low, high, bank = slice(0, CH), slice(CH, P), unit_bank(b, n)
                even, odd = k_hi[buf] if n < KT else q_st[buf]
                for dst, at in ((even, low), (odd, high)):
                    nc.scalar.activation(dst[at, :, j, :], bank[at, 0:2 * P].rearrange("p (i t) -> p i t", i=2),
                                         ACT.Identity, bias=qk_bias[at, qk_column(n):qk_column(n) + 1]
                                         ).then_inc(qk_hi_done, 1)

            def copy_x(b, k):
                n = STAT_SLOTS.index(k)
                act.wait_ge(xt_full, BLOCKS * (b + 1) + n + 1)
                if n % 2 == 0:
                    at_least(act, h_split, 2 * (PPB * b + n // 2 + 1))
                dst = xt_sb[:, n // 2, :, n % 2 * P:(n % 2 + 1) * P]
                nc.scalar.copy(dst, unit_bank(b, n).rearrange("p (j t) -> p j t", j=KT)).then_inc(xt_copied, 1)

            def norm_x(b, k, n):
                if k == 2 * 16 + 13:
                    act.wait_ge(affine_ready, b + 2)
                for ct in (2 * n, 2 * n + 1):
                    x_ct = xt_sb[:, (k // 16 + 2) % PPB, ct, :]
                    last = nc.scalar.activation(x_ct, x_ct, ACT.Identity,
                                                bias=x_add[:, ct:ct + 1], scale=x_mul[:, ct:ct + 1])
                last.then_inc(xt_normed, 1)

            def round_qkv_weights(t):
                act.wait_ge(w_loaded[t], 16)
                for part in range(3):
                    cols = slice(part * C, (part + 1) * C)
                    nc.scalar.activation(w_hi[:, t, cols], w_stage[t][:, cols], ACT.Identity,
                                         scale=CH ** -0.5 if part == 1 else 1.0).then_inc(w_rounded, 1)

            def round_proj_weights():
                act.wait_ge(pw_loaded, 16 * KT)
                for t in range(KT):
                    nc.scalar.copy(pw_hi[:, t, :], pw_stage[t]).then_inc(w_rounded, 1)

            def slot(b, k):
                s = SPB * b + k
                kind, n, _ = large_unit(k)
                if kind == "qk" and within(made_pair(b, k), N_PAIRS):
                    qk_hi(b, k, n)
                if within(s, N_SLOTS):
                    softmax_exp(b, k)
                if k % 4 == 0:
                    half, side = 2 * BLOCKS * b + k // 4 - 2, (k // 4) % 2
                    if within(half, N_HALVES):
                        act.wait_ge(pv_done, half + 1)
                        at_least(act, proj_full, BLOCKS * b + k // 8 - 2 + side)
                        nc.scalar.copy(attn_hi[:, attn_place(k // 8 + 1, side), :], pv_ps[:, side, :]
                                       ).then_inc(attn_hi_done, 1)
                if small_unit(k, 0)[0] == "stats" and within(b + 1, BATCHES):
                    copy_x(b, k)
                if within(s - 1, N_SLOTS):
                    n, query_tile = (k - 1) // 4, (k - 1) % 4
                    act.wait_ge(t_full, s)
                    if query_tile == 0:
                        at_least(act, pv_done, 2 * BLOCKS * b + n - 1)
                    nc.scalar.copy(probs_t[n % 2][:, :, query_tile, :], t_ps[:, :, :]).then_inc(t_taken, 1)
                if small_unit(k, 1)[0] == "stats" and within(b + 1, BATCHES):
                    copy_x(b, k)
                if before_start(b) and k in STAT_SLOTS[1::2]:
                    round_qkv_weights(STAT_SLOTS.index(k) // 2)
                if before_start(b) and k == STAT_SLOTS[-1]:
                    round_proj_weights()
                if k % 16 in (13, 14) and within(xt_pair(b, k), N_PAIRS):
                    norm_x(b, k, k % 16 - 13)

            for t in range(KT):
                act.dma_start(w_stage[t], qkv_w[t * P:(t + 1) * P, :]).then_inc(w_loaded[t], 16)
            for t in range(KT):
                act.dma_start(pw_stage[t], proj_w[t * P:(t + 1) * P, :]).then_inc(pw_loaded, 16)
            batches(act, slot)

        @block.vector
        def _(dve):
            def split_qkv_weights(t):
                for part in range(3):
                    cols = slice(part * C, (part + 1) * C)
                    dve.wait_ge(w_rounded, 3 * t + part + 1)
                    last = nc.vector.scalar_tensor_tensor(
                        w_lo[:, t, cols], w_stage[t][:, cols], CH ** -0.5 if part == 1 else 1.0,
                        w_hi[:, t, cols].bitcast(F32), ALU.mult, ALU.subtract)
                last.then_inc(w_ready, 1)

            def split_proj_weights():
                for t in range(KT):
                    dve.wait_ge(w_rounded, 3 * KT + t + 1)
                    nc.vector.tensor_tensor(pw_lo[:, t, :], pw_stage[t], pw_hi[:, t, :].bitcast(F32),
                                            ALU.subtract).then_inc(w_ready, 1)
                dve.wait_ge(const_loaded, 16 * 5)
                nc.vector.tensor_scalar(qk_bias[:, KT:2 * KT], qk_bias[:, KT:2 * KT], CH ** -0.5, None,
                                        ALU.mult).then_inc(bias_scaled, 1)

            def qk_split(b, k, n):
                g, buf, j = made_pair(b, k), (k // 16 + 1) % 2, n % KT
                low, high, bank = slice(0, CH), slice(CH, P), unit_bank(b, n)
                if n >= KT:
                    places = ((q_st[buf][0], high, low, q_st[buf][0]), (q_st[buf][1], low, high, q_st[buf][1]))
                else:
                    places = ((k_lo[buf][0], low, low, k_hi[buf][0]), (k_lo[buf][1], high, high, k_hi[buf][1]))
                for half, (dst, to, of, hi) in enumerate(places):
                    dve.wait_ge(qk_hi_done, 2 * (2 * KT * g + n) + half + 1)
                    last = nc.vector.scalar_tensor_tensor(
                        dst[to, :, j, :], bank[of, 0:2 * P].rearrange("p (i t) -> p i t", i=2),
                        qk_bias[of, qk_column(n):qk_column(n) + 1],
                        hi[of, :, j, :].bitcast(F32), ALU.add, ALU.subtract)
                last.then_inc(qk_ready, 1)

            def slot(b, k):
                s = SPB * b + k
                if within(s - 1, N_SLOTS):
                    dve.wait_ge(probs_ready, s)
                    nc.vector.reciprocal(inv_sum[:, :], row_sum[:, (k - 1) % 2:(k - 1) % 2 + 1]).then_inc(inv_ready, 1)
                    dve.wait_ge(inv_ready, s)
                    p = probs[(k - 1) % 2]
                    nc.vector.tensor_scalar(p[:, :], p[:, :], inv_sum[:, :], None, ALU.mult).then_inc(probs_scaled, 1)
                if within(s, N_SLOTS):
                    dve.wait_ge(scores_full, s + 1)
                    nc.vector.tensor_reduce(neg_max[:, k % 4:k % 4 + 1], s_ps[k % 2][:, :], AX.X, ALU.max,
                                            negate=True).then_inc(max_ready, 1)
                kind, n, part = large_unit(k)
                if kind == "qk" and within(made_pair(b, k), N_PAIRS):
                    qk_split(b, k, n)
                if kind == "v" and part == 1 and within(made_pair(b, k), N_PAIRS):
                    g = made_pair(b, k)
                    dve.wait_ge(v_full, 2 * g + n + 1)
                    if n == 0 and within(g - 2, N_PAIRS):
                        dve.wait_ge(pv_done, 4 * (g - 1))
                    nc.vector.tensor_tensor(v_sb[(k // 16 + 1) % 2][:, n, :], c_ps[:, :], v_bias[:, :],
                                            ALU.add).then_inc(v_ready, 1)
                if kind == "proj" and part == 1:
                    h, n = proj_block(b, k), k // 8 - 2
                    if within(h, N_BLOCKS):
                        dve.wait_ge(proj_full, h + 1)
                        if n % 2 == 0:
                            dve.wait_ge(residual_ready, PPB * b + n // 2 + 1)
                        r = x_pair[:, (n // 2) % XRING, n % 2, :]
                        nc.vector.tensor_tensor(r, c_ps[:, :], r, ALU.add).then_inc(out_ready, 1)
                statistics(b, k)
                if before_start(b) and k - 1 in STAT_SLOTS[1::2]:
                    split_qkv_weights(STAT_SLOTS.index(k - 1) // 2)
                if before_start(b) and k == GROUP_VAR_SLOT:
                    split_proj_weights()
                if k % 4 == 0:
                    half, side = 2 * BLOCKS * b + k // 4 - 2, (k // 4) % 2
                    if within(half, N_HALVES):
                        dve.wait_ge(attn_hi_done, half + 1)
                        hi, lo = (a[:, attn_place(k // 8 + 1, side), :] for a in (attn_hi, attn_lo))
                        nc.vector.tensor_tensor(lo, pv_ps[:, side, :], hi.bitcast(F32),
                                                ALU.subtract).then_inc(attn_ready, 1)

            def statistics(b, k):
                if not within(b + 1, BATCHES):
                    return
                nb = b + 1
                if k - 1 in STAT_SLOTS:
                    u = STAT_SLOTS.index(k - 1)
                    dve.wait_ge(xt_copied, BLOCKS * nb + u + 1)
                    if u == 0:
                        at_least(dve, aggregated, 2 * nb)
                    for t in range(KT):
                        last = nc.vector.bn_stats(bn[:, t, u, :], xt_sb[:, u // 2, t, u % 2 * P:(u % 2 + 1) * P])
                    last.then_inc(bn_done, 1)
                if k == AGGREGATE_SLOT:
                    at_least_aside(dve, bn_done, BLOCKS * (nb + 1))
                    for t in range(KT):
                        last = nc.vector.bn_aggr(mv[:, t, :], bn[:, t, :, :].rearrange("p u s -> p (u s)"))
                    last.then_inc(aggregated, 1)
                if k == GROUP_MEAN_SLOT:
                    dve.wait_ge(group_full, 2 * nb + 1)
                    at_least(dve, affine_ready, nb)
                    nc.vector.tensor_copy(gmv[:, :, :].rearrange("p t s -> p (t s)"), c_ps[:, 0:2 * KT]).then_inc(group_taken, 1)
                    dve.wait_ge(group_taken, 2 * nb + 1)
                    nc.vector.tensor_tensor(dmean[:, :], mv[:, :, 0], gmv[:, :, 0], ALU.subtract).then_inc(mean_off, 1)
                    dve.wait_ge(mean_off, nb + 1)
                    nc.vector.tensor_tensor(dsq[:, :], dmean[:, :], dmean[:, :], ALU.mult).then_inc(aggregated, 1)
                if k == GROUP_VAR_SLOT:
                    dve.wait_ge(group_full, 2 * nb + 2)
                    nc.vector.scalar_tensor_tensor(gvar[:, :], c_ps[:, 0:KT], EPS, gmv[:, :, 1],
                                                   ALU.add, ALU.add).then_inc(group_taken, 1)

            batches(dve, slot)

        @block.gpsimd
        def _(pool):
            def broadcast_row(row):
                return row.rearrange("(a n) -> a n", a=1).broadcast_to([P, C])

            nc.gpsimd.memset(ident[:, :], 0.0).then_inc(pool_chain, 1)
            nc.gpsimd.memset(group_avg[:, :], 1.0 / GROUP).then_inc(pool_chain, 1)
            nc.gpsimd.memset(half_neg[:, :], -0.5).then_inc(pool_chain, 1)
            pool.wait_ge(pool_chain, 3)
            nc.gpsimd.affine_select(out=ident[:, :], in_=ident[:, :], compare_op=ALU.not_equal, fill=1.0, base=0,
                                    pattern=[[-1, P]], channel_multiplier=1).then_inc(const_made, 1)
            groups = group_avg[:, :].rearrange("p (g c) -> p g c", c=GROUP)
            nc.gpsimd.affine_select(out=groups, in_=groups, compare_op=ALU.is_ge, fill=0.0, base=0,
                                    pattern=[[-GROUP, P // GROUP], [0, GROUP]], channel_multiplier=1).then_inc(pool_chain, 1)
            pool.wait_ge(pool_chain, 4)
            nc.gpsimd.affine_select(out=groups, in_=groups, compare_op=ALU.is_ge, fill=0.0, base=GROUP - 1,
                                    pattern=[[GROUP, P // GROUP], [0, GROUP]], channel_multiplier=-1).then_inc(const_made, 1)
            pool.dma_start(v_bias[:, :], broadcast_row(qkv_b[2 * C:3 * C])).then_inc(const_loaded, 16)
            pool.dma_start(p_bias[:, :], broadcast_row(proj_b)).then_inc(const_loaded, 16)
            with nc.allow_non_contiguous_dma("vectors to the partitions, once"):
                pool.dma_start(qk_bias[:, :], qkv_b[0:2 * C].rearrange("(j p) -> p j", p=P)).then_inc(const_loaded, 16)
                pool.dma_start(n_scale[:, :], norm_scale.rearrange("(j p) -> p j", p=P)).then_inc(const_loaded, 16)
                pool.dma_start(n_bias[:, :], norm_bias.rearrange("(j p) -> p j", p=P)).then_inc(const_loaded, 16)
            pool.wait_ge(const_loaded, 16 * 5)

            def split_h(b, k):
                g = xt_pair(b, k)
                at_least_aside(pool, v_full, 2 * g)
                for n in range(2):
                    part = slice(2 * n, 2 * n + 2)
                    h = xt_sb[:, (k // 16 + 2) % PPB, part, :]
                    at_least_aside(pool, xt_normed, 2 * g + n + 1)
                    nc.gpsimd.tensor_copy(h_hi[:, part, :], h).then_inc(h_rounded, 1)
                    pool.wait_ge(h_rounded, 2 * g + n + 1)
                    nc.gpsimd.tensor_tensor(h_lo[:, part, :], h, h_hi[:, part, :].bitcast(F32),
                                            ALU.subtract).then_inc(h_split, 1)

            def affine(b):
                nb = b + 1
                pool.wait_ge(group_taken, 2 * nb + 2)
                nc.gpsimd.tensor_tensor(rstd[:, :], gvar[:, :], half_neg[:, :], ALU.pow).then_inc(affine_step, 1)
                at_least(pool, xt_normed, 2 * PPB * nb)
                pool.wait_ge(affine_step, 3 * nb + 1)
                nc.gpsimd.tensor_tensor(x_mul[:, :], rstd[:, :], n_scale[:, :], ALU.mult).then_inc(affine_step, 1)
                pool.wait_ge(affine_step, 3 * nb + 2)
                nc.gpsimd.tensor_tensor(mean_a[:, :], gmv[:, :, 0], x_mul[:, :], ALU.mult).then_inc(affine_step, 1)
                pool.wait_ge(affine_step, 3 * nb + 3)
                nc.gpsimd.tensor_tensor(x_add[:, :], n_bias[:, :], mean_a[:, :], ALU.subtract).then_inc(affine_ready, 1)

            def slot(b, k):
                if k % 16 == 15 and within(xt_pair(b, k), N_PAIRS):
                    split_h(b, k)
                if k % 16 == 7:
                    g, n = attended_pair(b, k), k // 16
                    if within(g, N_PAIRS):
                        pool.wait_ge(x_loaded[n % XRING], 16 * (PPB // XRING * b + n // XRING + 1))
                        for i in range(2):
                            r = x_pair[:, n % XRING, i, :]
                            last = nc.gpsimd.tensor_tensor(r, r, p_bias[:, :], ALU.add)
                        last.then_inc(residual_ready, 1)
                if k == GROUP_VAR_SLOT and within(b + 1, BATCHES):
                    affine(b)

            batches(pool, slot)


_INS = ["x", "L0_conv_norm_scale", "L0_conv_norm_bias", "L0_conv_qkv_w", "L0_conv_qkv_b", "L0_conv_proj_w",
        "L0_conv_proj_b"]


def kernel(**inputs):
    import numpy as np
    import concourse.bacc as bacc
    from concourse.bass_utils import run_bass_kernel_spmd

    nc = bacc.Bacc("TRN2", target_bir_lowering=False, num_devices=1)
    arrays, args = {}, []
    for name in _INS:
        a = np.ascontiguousarray(inputs[name])
        arrays[f"in_{name}"] = a
        args.append(nc.dram_tensor(f"in_{name}", a.shape, F32, kind="ExternalInput").ap())
    result = nc.dram_tensor("result", arrays["in_x"].shape, F32, kind="ExternalOutput").ap()
    attention_block(nc, *args, result)
    run = run_bass_kernel_spmd(nc, [arrays], core_ids=[0])
    return run.results[0]["result"]
```
